# Optimizing a Trainium2 kernel written in Bass

```python
import numpy as np
import jax
import jax.numpy as jnp

def _softmax(x, axis=-1):
    return jax.nn.softmax(x, axis=axis)

def _gelu(x):
    return jax.nn.gelu(x, approximate=True)

def _silu(x):
    return jax.nn.silu(x)

def _sigmoid(x):
    return jax.nn.sigmoid(x)

def _layernorm(x, axis=-1, eps=1e-05):
    m = jnp.mean(x, axis=axis, keepdims=True)
    v = jnp.var(x, axis=axis, keepdims=True)
    return (x - m) / jnp.sqrt(v + eps)

def _scatter_add(tgt, idx, src, axis=0):
    return tgt.at[idx].add(src)

def _segment_sum(src, seg, n):
    return jax.ops.segment_sum(src, seg, n)
kernel_name = 'mk_vit_tower_d1_tok_img768_r4_a660a4'

def setup_inputs(seed: int=0):
    np.random.seed(seed)
    _w = jnp.asarray

    def _rec_inputs():
        import jax
        import jax.numpy as jnp
        _rk = jax.random.key(seed)
        x = -0.00016672 + 0.999947 * jax.random.normal(jax.random.fold_in(_rk, 1), (64, 3, 96, 96), jnp.float32)
        return x
    x = _rec_inputs()

    def _L0_tok_setup():
        import jax, jax.numpy as jnp
        import numpy as np
        P = 16
        EMBED_DIM = 192
        key = jax.random.key(seed)
        k1, k2 = jax.random.split(key)
        x = jax.random.normal(k1, (64, 3, 96, 96), dtype=jnp.float32)
        W = jax.random.normal(k2, (3 * P * P, EMBED_DIM), dtype=jnp.float32) * (1.0 / np.sqrt(3 * P * P))
        return {'x': x, 'W': W}
    _L0_tok_all = _L0_tok_setup()
    _L0_tok_in = {k: v for k, v in _L0_tok_all.items() if k in ('W',)}
    del _L0_tok_all

    def _L0_attn_setup():
        import jax, jax.numpy as jnp
        import numpy as np
        import math
        N_EMBED = 192
        N_HEAD = 12
        BLOCK_SIZE = 512
        B, T = (4, 512)
        key = jax.random.key(seed)
        ks = jax.random.split(key, 5)
        x = jax.random.normal(ks[0], (B, T, N_EMBED), dtype=jnp.float32)
        s = 1.0 / math.sqrt(N_EMBED)
        W_attn = jax.random.uniform(ks[1], (3 * N_EMBED, N_EMBED), minval=-s, maxval=s, dtype=jnp.float32)
        b_attn = jax.random.uniform(ks[2], (3 * N_EMBED,), minval=-s, maxval=s, dtype=jnp.float32)
        W_o = jax.random.uniform(ks[3], (N_EMBED, N_EMBED), minval=-s, maxval=s, dtype=jnp.float32)
        b_o = jax.random.uniform(ks[4], (N_EMBED,), minval=-s, maxval=s, dtype=jnp.float32)
        return {'x': x, 'W_attn': W_attn, 'b_attn': b_attn, 'W_o': W_o, 'b_o': b_o}
    _L0_attn_all = _L0_attn_setup()
    _L0_attn_in = {k: v for k, v in _L0_attn_all.items() if k in ('W_attn', 'b_attn', 'W_o', 'b_o')}
    del _L0_attn_all

    def _L0_ffn_setup():
        import jax, jax.numpy as jnp
        import numpy as np
        E, C, F, K = (8, 192, 768, 2)
        key = jax.random.key(seed)
        k0, k1, k2, k3 = jax.random.split(key, 4)
        B, T = (8, 512)
        return {'x': jax.random.normal(k0, (B, T, C), jnp.float32), 'router_w': jax.random.normal(k1, (E, C), jnp.float32) * 0.02, 'w1': jax.random.normal(k2, (E, C, F), jnp.float32) * 0.02, 'b1': jnp.zeros((E, F), jnp.float32), 'w2': jax.random.normal(k3, (E, F, C), jnp.float32) * 0.02, 'b2': jnp.zeros((E, C), jnp.float32)}
    _L0_ffn_all = _L0_ffn_setup()
    _L0_ffn_in = {k: v for k, v in _L0_ffn_all.items() if k in ('router_w', 'w1', 'b1', 'w2', 'b2')}
    del _L0_ffn_all
    return {'x': x, 'L0_tok_W': _L0_tok_in['W'], 'L0_attn_W_attn': _L0_attn_in['W_attn'], 'L0_attn_b_attn': _L0_attn_in['b_attn'], 'L0_attn_W_o': _L0_attn_in['W_o'], 'L0_attn_b_o': _L0_attn_in['b_o'], 'L0_ffn_router_w': _L0_ffn_in['router_w'], 'L0_ffn_w1': _L0_ffn_in['w1'], 'L0_ffn_b1': _L0_ffn_in['b1'], 'L0_ffn_w2': _L0_ffn_in['w2'], 'L0_ffn_b2': _L0_ffn_in['b2']}

def reference(x, L0_tok_W, L0_attn_W_attn, L0_attn_b_attn, L0_attn_W_o, L0_attn_b_o, L0_ffn_router_w, L0_ffn_w1, L0_ffn_b1, L0_ffn_w2, L0_ffn_b2):
    import jax
    import jax.numpy as jnp

    def _L0_tok_ref(x, W):
        import jax, jax.numpy as jnp
        import numpy as np
        P = 16
        EMBED_DIM = 192
        B, C, H, Wd = x.shape
        xp = x.reshape(B, C, H // P, P, Wd // P, P)
        xp = jnp.transpose(xp, (0, 2, 4, 3, 5, 1))
        xp = xp.reshape(B, H // P * (Wd // P), P * P * C)
        return jnp.einsum('bnd,de->bne', xp, W)

    def _L0_attn_ref(x, W_attn, b_attn, W_o, b_o):
        import jax, jax.numpy as jnp
        import numpy as np
        import math
        N_EMBED = 192
        N_HEAD = 12
        BLOCK_SIZE = 512
        B, T = (4, 512)
        Bsz, Tlen, C = x.shape
        hd = C // N_HEAD
        qkv = x @ W_attn.T + b_attn
        q, k, v = jnp.split(qkv, 3, axis=2)
        q = q.reshape(Bsz, Tlen, N_HEAD, hd).transpose(0, 2, 1, 3)
        k = k.reshape(Bsz, Tlen, N_HEAD, hd).transpose(0, 2, 1, 3)
        v = v.reshape(Bsz, Tlen, N_HEAD, hd).transpose(0, 2, 1, 3)
        att = jnp.einsum('bhqd,bhkd->bhqk', q, k) * (1.0 / math.sqrt(hd))
        causal = jnp.tril(jnp.ones((Tlen, Tlen), dtype=bool))
        att = jnp.where(causal[None, None], att, -jnp.inf)
        att = jax.nn.softmax(att, axis=-1)
        y = jnp.einsum('bhqk,bhkd->bhqd', att, v)
        y = y.transpose(0, 2, 1, 3).reshape(Bsz, Tlen, C)
        return y @ W_o.T + b_o

    def _L0_ffn_ref(x, router_w, w1, b1, w2, b2):
        import jax, jax.numpy as jnp
        import numpy as np
        E, C, F, K = (8, 192, 768, 2)
        B, T, Cc = x.shape
        flat = x.reshape(-1, Cc)
        logits = flat @ router_w.T
        probs = jax.nn.softmax(logits.astype(jnp.float32), axis=-1)
        top_w, top_i = jax.lax.top_k(probs, K)
        top_w = (top_w / top_w.sum(-1, keepdims=True)).astype(x.dtype)
        out = jnp.zeros_like(flat)
        for e in range(E):
            w_e = jnp.sum(top_w * (top_i == e), axis=-1)[:, None]
            h = jax.nn.gelu(flat @ w1[e] + b1[e], approximate=False)
            out = out + w_e * (h @ w2[e] + b2[e])
        return out.reshape(B, T, Cc)
    h = _L0_tok_ref(x, L0_tok_W)
    h = h + _L0_attn_ref(_layernorm(h, axis=-1), L0_attn_W_attn, L0_attn_b_attn, L0_attn_W_o, L0_attn_b_o)
    h = h + _L0_ffn_ref(_layernorm(h, axis=-1), L0_ffn_router_w, L0_ffn_w1, L0_ffn_b1, L0_ffn_w2, L0_ffn_b2)
    return h

_drawn_inputs = setup_inputs


def setup_inputs(seed=0):
    import zlib

    import numpy as np

    out = dict(_drawn_inputs(seed))
    spreads = {'L0_ffn_b1': (0.0, 0.374), 'L0_ffn_b2': (0.0, 0.1)}
    factors = {}
    for name, (base, spread) in spreads.items():
        noise = np.random.default_rng([zlib.crc32(name.encode()), seed]).standard_normal(out[name].shape)
        drawn = base * np.exp(spread * noise) if base else spread * noise
        out[name] = jnp.asarray(drawn.astype(out[name].dtype))
    for name, factor in factors.items():
        out[name] = (out[name] * factor).astype(out[name].dtype)
    return out
```

```python
from contextlib import ExitStack

import numpy as np
import concourse.bass as bass
from concourse import mybir

F32 = mybir.dt.float32
F16 = mybir.dt.float16
BF16 = mybir.dt.bfloat16
U32 = mybir.dt.uint32
ALU = mybir.AluOpType
ACT = mybir.ActivationFunctionType
AX = mybir.AxisListType

B, CIN, IMG, PATCH = 64, 3, 96, 16
SIDE = IMG // PATCH
T = SIDE * SIDE
C, HEADS = 192, 12
HD = C // HEADS
E, F = 8, 768
DTOK = CIN * PATCH * PATCH
KT = DTOK // 128

TI = 3
TT = TI * T
NT = -(-B // TI)
HC = C // 2
HH = HEADS // 2
GH = 3
NG = HEADS // GH
KEYS = GH * T
GC = GH * HD
VC = GC + GH
FC = F // 128
LAST = B * T - (NT - 1) * TT

S_X, S_W = 2.0 ** 8, 2.0 ** 10
S_XW = S_X * S_W
S_Q, S_V, S_P, S_G = 2.0 ** 6, 2.0 ** 8, 2.0 ** 12, 2.0 ** 6
EPS = 1e-5
PRODUCTS = [(0, 0), (0, 1), (1, 0)]

CR = 2


def DONE(t):
    return t + 1 + CR


def FREE2(t):
    return t + 1


def FREE1(t):
    return t + CR


def build(nc, xt, wtok, wqkv, wo, wr, w1, w2, b2, idf, idh, selq, causal, selv, hmask, vmask, vones, eid, out):
    ds = bass.ds
    ctx = ExitStack()
    with ctx:
        def sb(name, shape, dt=F32):
            return ctx.enter_context(nc.sbuf_tensor(name, shape, dt))

        def sem(name):
            return ctx.enter_context(nc.semaphore(name))

        H = sb("H", [TT, NT * C])
        XN = sb("XN", [HC + 1, NT * 4 * TT], F16)
        W1 = [sb(f"W1{p}", [HC + 1, E * 2 * F], F16) for p in "hl"]
        W2 = [sb(f"W2{p}", [128, E * FC * C], F16) for p in "hl"]
        B2 = [sb(f"B2{p}", [1, E * C], F16) for p in "hl"]
        LG = sb("LG", [TT, NT * E])
        ST = sb("ST", [TT, NT * 6])
        MEAN = sb("MEAN", [TT, NT])
        VAR = sb("VAR", [TT, NT])
        DM = sb("DM", [TT, NT])
        SCALE = sb("SCALE", [128, 1])
        RS = sb("RS", [TT, NT])
        EPSV = sb("EPSV", [TT, 1])
        ONE = sb("ONE", [1, 128], F16)
        IDF = sb("IDF", [128, 128])
        IDH = sb("IDH", [128, 128], F16)
        SELQ = sb("SELQ", [T, TT], BF16)
        CAUS = sb("CAUS", [T, T], BF16)
        SELV = sb("SELV", [TT, TI * KEYS], F16)
        HM = sb("HM", [HC, HH * TT], F16)
        VM = sb("VM", [KEYS, C])
        VO = sb("VO", [KEYS, GH], F16)
        EID = sb("EID", [TT, E])
        WA = [sb(f"WA{p}", [HC + 1, 2 * 3 * C], F16) for p in "hl"]
        WO = [sb(f"WO{p}", [HC + 1, 2 * C], F16) for p in "hl"]
        WR = [sb(f"WR{p}", [HC, 2 * E], F16) for p in "hl"]
        WSTG = sb("WSTG", [128, 2 * F])
        REG = sb("REG", [128, max(6 * KT * TT, NT * C)])
        XW = KT * TT
        XHL = REG[:, 4 * XW:6 * XW].bitcast(F16)
        Y = [REG[0:TT, p * NT * C // 2:(p + 1) * NT * C // 2].bitcast(F16) for p in range(2)]
        KW = 2 * HH * TT
        KBR = sb("KBR", [128, 2 * KW])
        KB = [KBR[0:HC, p * KW:(p + 1) * KW].bitcast(F16) for p in range(2)]
        WT = [KBR[:, p * KT * C // 2:(p + 1) * KT * C // 2].bitcast(F16) for p in range(2)]
        DW = TI * (TT + T)
        PTR = sb("PTR", [128, 2 * NG * DW])
        PT = [PTR[0:KEYS, p * NG * DW:(p + 1) * NG * DW].bitcast(F16) for p in range(2)]
        SMALL = [(wtok, WT, 128, KT * C), (wqkv, WA, HC + 1, 6 * C), (wo, WO, HC + 1, 2 * C), (wr, WR, HC, 2 * E)]
        RAW, at = [], 0
        for _, _, rows, cols in SMALL:
            RAW.append(PTR[0:rows, at:at + cols])
            at += cols
        G = PTR[:, 0:2 * FC * TT]
        GP = [PTR[:, (2 + p) * FC * TT:(3 + p) * FC * TT].bitcast(F16) for p in range(2)]
        XF = sb("XF", [TT, 2 * C])
        XP = sb("XP", [TT, 2 * 2 * C], F16)
        QM = [sb(f"QM{p}", [HC, 2 * 2 * DW], F16) for p in "hl"]
        KP = [sb(f"KP{p}", [HC, 2 * 2 * TT], F16) for p in "hl"]
        VP = [sb(f"VP{p}", [TT, 2 * C], F16) for p in "hl"]
        VB = [sb(f"VB{p}", [KEYS, 2 * TI * NG * VC], F16) for p in "hl"]
        MX = sb("MX", [TT, 2 * HEADS])
        PR = sb("PR", [TT, 2 * HEADS * T])
        RD = sb("RD", [TT, 2 * HEADS])
        YF = sb("YF", [TT, 2 * C])
        YT = sb("YT", [HC + 1, 2 * 4 * TT], F16)
        M8 = PR[:, 0:NT * E]
        I8 = PR[:, NT * E:2 * NT * E].bitcast(U32)
        OH = [WSTG[0:TT, n * NT * E:(n + 1) * NT * E] for n in range(2)]
        GW = WSTG[0:TT, 2 * NT * E:3 * NT * E]
        RT = WSTG[0:TT, 3 * NT * E:3 * NT * E + 6 * NT]

        PSA = ctx.enter_context(nc.psum_tensor("PSA", [128, 8 * 512], F32))

        def bank(n, rows, cols, dt=F32):
            v = PSA[0:rows, n * 512:(n + 1) * 512]
            return (v.bitcast(dt) if dt != F32 else v)[:, 0:cols]

        const_in, consts_set = sem("const_in"), sem("consts_set")
        raw_in = [sem(f"raw_in{n}") for n in range(4)]
        small_hi, small_lo = sem("small_hi"), sem("small_lo")
        pt_zero = sem("pt_zero")
        x_in = [sem(f"x_in{n}") for n in range(2)]
        xh_done, xl_done, emb_mm, h_done = [sem(n) for n in ("xh_done", "xl_done", "emb_mm", "h_done")]
        st_done, mv_done, sd_done, rs_done = [sem(n) for n in ("st_done", "mv_done", "sd_done", "rs_done")]
        N1 = [sem(f"norm1_{n}") for n in ("row", "hi", "lo", "transposed", "done")]
        qk_mm, v_mm = sem("qk_mm"), sem("v_mm")
        qh_done, kh_done, vh_done = sem("qh_done"), sem("kh_done"), sem("vh_done")
        ql_done, kl_done, vl_done = sem("ql_done"), sem("kl_done"), sem("vl_done")
        kbh_done, kbl_done = sem("kbh_done"), sem("kbl_done")
        s_mm, mx_done, sub_done, p_done = sem("s_mm"), sem("mx_done"), sem("sub_done"), sem("p_done")
        pt_mm, pth_done, ptl_done = sem("pt_mm"), sem("pth_done"), sem("ptl_done")
        vr_mm, vbh_done, vbl_done = sem("vr_mm"), sem("vbh_done"), sem("vbl_done")
        o_mm, rd_done, yf_done, yh_done, yl_done = [sem(n) for n in ("o_mm", "rd_done", "yf_done", "yh_done", "yl_done")]
        yt_mm, yt_done, op_mm, h2_done, st2_done, mv2_done = [sem(n) for n in ("yt_mm", "yt_done", "op_mm", "h2_done", "st2_done", "mv2_done")]
        sd2_done, rs2_done = sem("sd2_done"), sem("rs2_done")
        N2 = [sem(f"norm2_{n}") for n in ("row", "hi", "lo", "transposed", "done")]
        r_mm, lg_done = sem("r_mm"), sem("lg_done")
        route, gap_exp = sem("route"), sem("gap_exp")
        b2_in = sem("b2_in")
        w_in = [sem(f"w_in{n}") for n in range(2)]
        w_scaled, w_hi, w_lo = sem("w_scaled"), sem("w_hi"), sem("w_lo")
        up_mm, gelu_done, gh_done, gl_done, down_mm, acc_done = [sem(n) for n in ("up_mm", "gelu_done", "gh_done", "gl_done", "down_mm", "acc_done")]
        stored = sem("stored")
        CONSTS = [(IDF, idf), (IDH, idh), (SELQ, selq), (CAUS, causal), (SELV, selv), (HM, hmask), (VM, vmask), (VO, vones), (EID, eid)]
        FILLS = 12
        block = ctx.enter_context(nc.Block())

        def xs(slot, k):
            return REG[:, (2 * slot + k) * XW:(2 * slot + k + 1) * XW]

        def xhl(u, p):
            return XHL[:, (2 * u + p) * XW:(2 * u + p + 1) * XW]

        def htile(t):
            return H[:, ds(t * C, C)]

        def xn(t, p, c):
            return XN[:, ds(t * (4 * TT) + (2 * p + c) * TT, TT)]

        def diag(buf, u, n):
            return buf[:, u * n * DW:(u + 1) * n * DW].rearrange("p (b q) -> p b q", q=TT + T)[:, :, 0:T]

        def kbd(p, u):
            return KB[p][:, u * KW:(u + 1) * KW]

        def vbd(p, u):
            return VB[p][:, u * TI * NG * VC:(u + 1) * TI * NG * VC]

        def heads(ap):
            return ap.rearrange("p (h k) -> p h k", h=HEADS)

        PIECES = 2 * E

        @block.sync
        def _(sp):
            def patches(pair, slot):
                sp.dma_start(REG[:, slot * 2 * XW:(slot + 1) * 2 * XW].rearrange("p (t c) -> p t c", t=2),
                             xt[ds(pair * 2, 2), :, :].rearrange("t p c -> p t c")).then_inc(x_in[slot], 16)

            sp.dma_start(RAW[0], wtok).then_inc(raw_in[0], 16)
            patches(0, 0)
            patches(1, 1)
            for n in range(1, len(SMALL)):
                sp.dma_start(RAW[n], SMALL[n][0]).then_inc(raw_in[n], 16)
            for dst, src in CONSTS:
                sp.dma_start(dst[:, :], src).then_inc(const_in, 16)
            sp.dma_start(WSTG[0:1, :], b2).then_inc(b2_in, 16)
            LOOPED = (NT // 2 - 3) // 2
            with sp.Fori(0, LOOPED) as i:
                for slot in range(2):
                    sp.wait_ge(xl_done, i * 4 + (2 * slot + 2 + CR))
                    patches(i * 2 + (2 + slot), slot)
            for pair in range(2 + 2 * LOOPED, NT // 2):
                sp.wait_ge(xl_done, 2 * (pair - 1) + CR)
                patches(pair, pair % 2)
            with sp.Fori(0, PIECES // 2) as i:
                for u in range(2):
                    sp.wait_ge(w_lo, i * 2 + (u + 1))
                    sp.dma_start(WSTG[0:HC + 1, u * F:(u + 1) * F], w1[:, ds((i * 2 + u) * F, F)]).then_inc(w_in[u], 16)
            with sp.Fori(0, PIECES // 2) as i:
                for u in range(2):
                    sp.wait_ge(w_lo, i * 2 + (PIECES + u + 1))
                    sp.dma_start(WSTG[:, u * F:u * F + FC * C // 2], w2[:, ds((i * 2 + u) * (FC * C // 2), FC * C // 2)]).then_inc(w_in[u], 16)
            of = out.rearrange("b t c -> (b t) c")
            with sp.Fori(0, NT - 1) as t:
                sp.wait_ge(acc_done, t + ((E - 1) * NT + 1 + CR))
                sp.dma_start(of[ds(t * TT, TT), :], htile(t)).then_inc(stored, 16)
            sp.wait_ge(acc_done, E * NT + CR)
            sp.dma_start(of[(NT - 1) * TT:B * T, :], H[0:LAST, (NT - 1) * C:NT * C]).then_inc(stored, 16)
            sp.wait_ge(stored, 16 * NT)

        @block.gpsimd
        def _(gp):
            for s in (kbl_done, yl_done):
                gp.sem_inc(s, CR)
            fills = [(EPSV[:, :], EPS / S_X ** 2), (ONE[:, :], S_G), (SCALE[:, :], S_W), (XN[HC:HC + 1, :], 0.0),
                     (XN[HC:HC + 1, :].rearrange("p (t c) -> p t c", t=NT)[:, :, 0:2 * TT], S_X),
                     (YT[HC:HC + 1, :], 0.0), (YT[HC:HC + 1, :].rearrange("p (t c) -> p t c", t=2)[:, :, 0:2 * TT], S_X)]
            fills += [(buf[p][:, :], 0.0) for buf in (QM, VB) for p in range(2)]
            for n, (dst, value) in enumerate(fills):
                if n:
                    gp.wait_ge(consts_set, n)
                nc.gpsimd.memset(dst, value).then_inc(consts_set, 1)
            gp.wait_ge(consts_set, len(fills))
            gp.wait_ge(const_in, 16 * len(CONSTS))
            nc.gpsimd.tensor_copy(VB[0][:, :].rearrange("p (n c) -> p n c", c=VC)[:, :, GC:VC],
                                  VO[:, :].unsqueeze(1).to_broadcast([KEYS, 2 * TI * NG, GH])).then_inc(consts_set, 1)
            gp.wait_ge(consts_set, FILLS)
            gp.wait_ge(small_lo, len(SMALL))
            nc.gpsimd.memset(PTR[:, :], 0.0).then_inc(pt_zero, 1)

            def split_w(n, raw, parts):
                nc.gpsimd.tensor_tensor(raw, raw, SCALE[0:raw.shape[0], 0:1].to_broadcast([raw.shape[0], raw.shape[1]]),
                                        ALU.mult).then_inc(w_scaled, 1)
                gp.wait_ge(w_scaled, n + 1)
                nc.gpsimd.tensor_copy(parts[0], raw).then_inc(w_hi, 1)
                gp.wait_ge(w_hi, n + 1)
                nc.gpsimd.tensor_tensor(parts[1], raw, parts[0], ALU.subtract).then_inc(w_lo, 1)

            gp.wait_ge(b2_in, 16)
            split_w(0, WSTG[0:1, :], [B2[p][:, :] for p in range(2)])
            gp.wait_ge(w_lo, 1)
            gp.sem_inc(w_lo, 1)

            def w1_piece(i, u):
                gp.wait_ge(w_in[u], i * 16 + 16)
                at = (i * 2 + u) * F
                split_w(i * 2 + (u + 1), WSTG[0:HC + 1, u * F:(u + 1) * F], [W1[p][:, ds(at, F)] for p in range(2)])

            def w2_piece(i, u):
                gp.wait_ge(w_in[u], i * 16 + (16 + 16 * E))
                w = FC * C // 2
                at = (i * 2 + u) * w
                split_w(i * 2 + (u + 1 + PIECES), WSTG[:, u * F:u * F + w], [W2[p][:, ds(at, w)] for p in range(2)])

            def keys_low(t, u):
                gp.wait_ge(kl_done, DONE(t))
                gp.wait_ge(s_mm, FREE2(t))
                nc.gpsimd.tensor_tensor(
                    kbd(1, u).rearrange("p (c h k) -> p c h k", c=2, h=HH),
                    KP[1][:, u * 2 * TT:(u + 1) * 2 * TT].rearrange("p (c k) -> p c k", c=2).unsqueeze(2).to_broadcast([HC, 2, HH, TT]),
                    HM[:, :].rearrange("p (h k) -> p h k", h=HH).unsqueeze(1).to_broadcast([HC, 2, HH, TT]),
                    ALU.mult).then_inc(kbl_done, 1)

            def y_parts(t, u):
                gp.wait_ge(yf_done, DONE(t))
                yf = YF[:, u * C:(u + 1) * C]
                nc.gpsimd.tensor_copy(Y[0][:, ds(t * C, C)], yf).then_inc(yh_done, 1)
                gp.wait_ge(yh_done, t + 1)
                nc.gpsimd.tensor_tensor(Y[1][:, ds(t * C, C)], yf, Y[0][:, ds(t * C, C)], ALU.subtract).then_inc(yl_done, 1)

            with gp.Fori(0, PIECES // 2) as i:
                for u in range(2):
                    w1_piece(i, u)
            keys_low(0, 0)
            keys_low(1, 1)
            with gp.Fori(0, (NT - 2) // 2) as i:
                for u in range(2):
                    t = i * 2 + (1 + u)
                    y_parts(t - 1, u)
                    keys_low(t + 1, u)
            y_parts(NT - 2, 0)
            y_parts(NT - 1, 1)
            with gp.Fori(0, PIECES // 2) as i:
                for u in range(2):
                    w2_piece(i, u)

        @block.scalar
        def _(act):
            for s in (xh_done, h_done, N1[1], N1[4], qh_done, kh_done, vh_done, p_done, pth_done, yt_done, N2[1], N2[4], gelu_done, gh_done):
                act.sem_inc(s, CR)
            for n, (_, parts, _, _) in enumerate(SMALL):
                act.wait_ge(raw_in[n], 16)
                nc.scalar.activation(parts[0][:, :], RAW[n], ACT.Copy, scale=S_W).then_inc(small_hi, 1)

            def patch_hi(t, u, slot, k, landed):
                act.wait_ge(x_in[slot], landed)
                act.wait_ge(emb_mm, FREE2(t))
                nc.scalar.activation(xhl(u, 0), xs(slot, k), ACT.Copy, scale=S_X).then_inc(xh_done, 1)

            def h_out(t, u):
                act.wait_ge(emb_mm, DONE(t))
                nc.scalar.activation(htile(t), bank(u, TT, C), ACT.Copy, scale=1 / S_XW).then_inc(h_done, 1)

            patch_hi(0, 0, 0, 0, 16)
            with act.Fori(0, (NT - 2) // 4) as i:
                for v in range(4):
                    t, ahead = i * 4 + v, v + 1
                    patch_hi(t + 1, ahead % 2, ahead // 2 % 2, ahead % 2, i * 16 + (16 if ahead < 4 else 32))
                    h_out(t, v % 2)
            patch_hi(NT - 1, 1, 0, 1, 16 * (NT // 4 + 1))
            h_out(NT - 2, 0)
            h_out(NT - 1, 1)

            def deviation(mv, done):
                act.wait_ge(mv, 6)
                nc.scalar.activation(RS[:, :], VAR[:, :], ACT.Sqrt, bias=EPSV[:, 0:1], scale=1 / (C * S_X ** 2)).then_inc(done, 1)

            def norm_hi(N, t, u):
                act.wait_ge(N[0], DONE(t))
                act.wait_ge(N[3], FREE2(t))
                nc.scalar.activation(XP[:, u * 2 * C:u * 2 * C + C], XF[:, u * C:(u + 1) * C], ACT.Copy).then_inc(N[1], 1)

            def norm_out(N, t, u):
                act.wait_ge(N[3], DONE(t))
                nc.scalar.activation(XN[0:HC, ds(t * (4 * TT), 4 * TT)], bank(2 + u, HC, 4 * TT, F16), ACT.Copy).then_inc(N[4], 1)

            def norm(N):
                norm_hi(N, 0, 0)
                with act.Fori(0, (NT - 2) // 2) as i:
                    for u in range(2):
                        norm_hi(N, i * 2 + (u + 1), 1 - u)
                        norm_out(N, i * 2 + u, u)
                norm_hi(N, NT - 1, 1)
                norm_out(N, NT - 2, 0)
                norm_out(N, NT - 1, 1)

            act.wait_ge(consts_set, 1)
            deviation(mv_done, sd_done)
            norm(N1)

            def qkv_hi(t, u):
                act.wait_ge(qk_mm, DONE(t))
                act.wait_ge(s_mm, FREE2(t))
                qk = bank(0, HC, 4 * TT)
                nc.scalar.activation(diag(QM[0], u, 2), qk[:, 0:2 * TT].rearrange("p (b q) -> p b q", q=T), ACT.Copy,
                                     scale=S_Q / S_XW).then_inc(qh_done, 1)
                act.wait_ge(kbh_done, FREE2(t))
                act.wait_ge(kbl_done, FREE2(t))
                nc.scalar.activation(KP[0][:, u * 2 * TT:(u + 1) * 2 * TT], qk[:, 2 * TT:4 * TT], ACT.Copy,
                                     scale=S_Q / S_XW).then_inc(kh_done, 1)
                act.wait_ge(v_mm, DONE(t))
                act.wait_ge(vr_mm, FREE2(t))
                nc.scalar.activation(VP[0][:, u * C:(u + 1) * C], bank(1, TT, C), ACT.Copy, scale=S_V / S_XW).then_inc(vh_done, 1)

            def exps(t, u):
                act.wait_ge(sub_done, DONE(t))
                pr = PR[:, u * HEADS * T:(u + 1) * HEADS * T]
                nc.scalar.activation(pr, pr, ACT.Exp, scale=HD ** -0.5 / S_Q ** 2).then_inc(p_done, 1)

            def probs_hi(t, u):
                act.wait_ge(pt_mm, DONE(t))
                act.wait_ge(o_mm, FREE2(t))
                nc.scalar.activation(diag(PT[0], u, NG), bank(3, KEYS, NG * TT).rearrange("p (b q) -> p b q", q=T), ACT.Copy,
                                     scale=S_P).then_inc(pth_done, 1)

            act.wait_ge(consts_set, FILLS)
            act.wait_ge(pt_zero, 1)
            qkv_hi(0, 0)
            exps(0, 0)
            qkv_hi(1, 1)
            probs_hi(0, 0)
            with act.Fori(0, (NT - 2) // 2) as i:
                for u in range(2):
                    t = i * 2 + (1 + u)
                    exps(t, 1 - u)
                    qkv_hi(t + 1, u)
                    probs_hi(t, 1 - u)
            exps(NT - 1, 1)
            probs_hi(NT - 1, 1)

            act.wait_ge(consts_set, FILLS)
            with act.Fori(0, NT // 2) as i:
                for u in range(2):
                    t = i * 2 + u
                    act.wait_ge(yt_mm, DONE(t))
                    act.wait_ge(op_mm, FREE2(t))
                    nc.scalar.activation(YT[0:HC, u * 4 * TT:(u + 1) * 4 * TT], bank(u, HC, 4 * TT, F16), ACT.Copy).then_inc(yt_done, 1)
            deviation(mv2_done, sd2_done)
            norm(N2)
            act.wait_ge(route, 3)
            nc.scalar.activation(RT[:, NT:2 * NT], RT[:, 0:NT], ACT.Exp, scale=1 / S_XW).then_inc(gap_exp, 1)
            with act.Fori(0, E * NT // 2) as i:
                for u in range(2):
                    n = i * 2 + u
                    g = G[:, u * FC * TT:(u + 1) * FC * TT]
                    act.wait_ge(up_mm, DONE(n))
                    act.wait_ge(gl_done, FREE2(n))
                    for half in range(2):
                        w = FC * TT // 2
                        ins = nc.scalar.activation(g[:, half * w:(half + 1) * w], bank(2 * u + half, 128, w), ACT.Gelu, scale=1 / S_XW)
                    ins.then_inc(gelu_done, 1)
                    act.wait_ge(gelu_done, DONE(n))
                    act.wait_ge(down_mm, FREE2(n))
                    nc.scalar.activation(GP[0][:, u * FC * TT:(u + 1) * FC * TT], g, ACT.Copy, scale=S_G).then_inc(gh_done, 1)

        @block.vector
        def _(dve):
            for s in (xl_done, st_done, N1[0], N1[2], ql_done, kl_done, vl_done, kbh_done, mx_done, sub_done,
                      ptl_done, vbl_done, rd_done, yf_done, h2_done, st2_done, N2[0], N2[2], lg_done, gl_done, acc_done):
                dve.sem_inc(s, CR)

            def low(dst, src, scale, hi):
                return nc.vector.scalar_tensor_tensor(dst, src, scale, hi, ALU.mult, ALU.subtract)

            for n, (_, parts, _, _) in enumerate(SMALL):
                dve.wait_ge(small_hi, n + 1)
                low(parts[1][:, :], RAW[n], S_W, parts[0][:, :]).then_inc(small_lo, 1)

            def patch_lo(t, u, slot, k):
                dve.wait_ge(xh_done, DONE(t))
                low(xhl(u, 1), xs(slot, k), S_X, xhl(u, 0)).then_inc(xl_done, 1)

            def stats(t, st):
                nc.vector.bn_stats(ST[:, ds(t * 6, 6)], htile(t)).then_inc(st, 1)

            def variances(st, mv):
                s = ST[:, :].rearrange("p (t c) -> p t c", c=6)
                dve.wait_ge(st, DONE(NT - 1))
                nc.vector.tensor_tensor(MEAN[:, :], s[:, :, 1], s[:, :, 4], ALU.add).then_inc(mv, 1)
                nc.vector.tensor_tensor(DM[:, :], s[:, :, 1], s[:, :, 4], ALU.subtract).then_inc(mv, 1)
                nc.vector.tensor_tensor(VAR[:, :], s[:, :, 2], s[:, :, 5], ALU.add).then_inc(mv, 1)
                dve.wait_ge(mv, 3)
                nc.vector.tensor_scalar(MEAN[:, :], MEAN[:, :], 0.5, None, ALU.mult).then_inc(mv, 1)
                nc.vector.scalar_tensor_tensor(DM[:, :], DM[:, :], 0.25 * C, DM[:, :], ALU.mult, ALU.mult).then_inc(mv, 1)
                dve.wait_ge(mv, 5)
                nc.vector.tensor_tensor(VAR[:, :], VAR[:, :], DM[:, :], ALU.add).then_inc(mv, 1)

            patch_lo(0, 0, 0, 0)
            patch_lo(1, 1, 0, 1)
            with dve.Fori(0, (NT - 2) // 4) as i:
                for v in range(4):
                    t, ahead = i * 4 + (1 + v), v + 2
                    dve.wait_ge(h_done, DONE(t - 1))
                    patch_lo(t + 1, ahead % 2, ahead // 2 % 2, ahead % 2)
                    stats(t - 1, st_done)
            dve.wait_ge(h_done, DONE(NT - 1))
            stats(NT - 2, st_done)
            stats(NT - 1, st_done)
            variances(st_done, mv_done)

            def norm_row(N, t, u):
                dve.wait_ge(N[2], FREE2(t))
                nc.vector.tensor_scalar(XF[:, u * C:(u + 1) * C], htile(t), MEAN[:, ds(t, 1)], RS[:, ds(t, 1)],
                                        ALU.subtract, ALU.mult).then_inc(N[0], 1)

            def norm_lo(N, t, u):
                dve.wait_ge(N[1], DONE(t))
                nc.vector.tensor_tensor(XP[:, u * 2 * C + C:(u + 1) * 2 * C], XF[:, u * C:(u + 1) * C],
                                        XP[:, u * 2 * C:u * 2 * C + C], ALU.subtract).then_inc(N[2], 1)

            def norm(N, sd, rs):
                dve.wait_ge(sd, 1)
                nc.vector.reciprocal(RS[:, :], RS[:, :]).then_inc(rs, 1)
                dve.wait_ge(rs, 1)
                norm_row(N, 0, 0)

            norm(N1, sd_done, rs_done)
            with dve.Fori(0, (NT - 2) // 2) as i:
                for u in range(2):
                    norm_row(N1, i * 2 + (u + 1), 1 - u)
                    norm_lo(N1, i * 2 + u, u)
            norm_row(N1, NT - 1, 1)
            norm_lo(N1, NT - 2, 0)
            norm_lo(N1, NT - 1, 1)

            def qkv_lo(t, u):
                dve.wait_ge(qh_done, DONE(t))
                dve.wait_ge(kh_done, DONE(t))
                qk = bank(0, HC, 4 * TT)
                low(diag(QM[1], u, 2), qk[:, 0:2 * TT].rearrange("p (b q) -> p b q", q=T), S_Q / S_XW, diag(QM[0], u, 2)).then_inc(ql_done, 1)
                kp = [KP[p][:, u * 2 * TT:(u + 1) * 2 * TT] for p in range(2)]
                low(kp[1], qk[:, 2 * TT:4 * TT], S_Q / S_XW, kp[0]).then_inc(kl_done, 1)
                dve.wait_ge(vh_done, DONE(t))
                low(VP[1][:, u * C:(u + 1) * C], bank(1, TT, C), S_V / S_XW, VP[0][:, u * C:(u + 1) * C]).then_inc(vl_done, 1)
                dve.wait_ge(s_mm, FREE2(t))
                nc.vector.tensor_tensor(
                    kbd(0, u).rearrange("p (c h k) -> p c h k", c=2, h=HH),
                    kp[0].rearrange("p (c k) -> p c k", c=2).unsqueeze(2).to_broadcast([HC, 2, HH, TT]),
                    HM[:, :].rearrange("p (h k) -> p h k", h=HH).unsqueeze(1).to_broadcast([HC, 2, HH, TT]),
                    ALU.mult).then_inc(kbh_done, 1)

            def shift(t, u):
                dve.wait_ge(s_mm, DONE(t))
                dve.wait_ge(sub_done, FREE2(t))
                mx = MX[:, u * HEADS:(u + 1) * HEADS]
                nc.vector.tensor_reduce(mx, heads(bank(2, TT, HEADS * T)), AX.X, ALU.max).then_inc(mx_done, 1)
                dve.wait_ge(mx_done, DONE(t))
                dve.wait_ge(pt_mm, FREE2(t))
                nc.vector.tensor_tensor(heads(PR[:, u * HEADS * T:(u + 1) * HEADS * T]), heads(bank(2, TT, HEADS * T)),
                                        mx.unsqueeze(2).to_broadcast([TT, HEADS, T]), ALU.subtract).then_inc(sub_done, 1)

            def values(t, u):
                dve.wait_ge(vr_mm, DONE(t))
                dve.wait_ge(o_mm, FREE2(t))
                for p, done in ((0, vbh_done), (1, vbl_done)):
                    nc.vector.tensor_tensor(
                        vbd(p, u).rearrange("p (b g c) -> p b g c", b=TI, g=NG)[:, :, :, 0:GC],
                        PSA[0:KEYS, 4 * 512:7 * 512].rearrange("p (b c) -> p b c", b=TI)[:, :, p * C:(p + 1) * C].rearrange("p b (g c) -> p b g c", g=NG),
                        VM[:, :].rearrange("p (g c) -> p g c", g=NG).unsqueeze(1).to_broadcast([KEYS, TI, NG, GC]),
                        ALU.mult).then_inc(done, 1)

            def probs_lo(t, u):
                dve.wait_ge(pth_done, DONE(t))
                low(diag(PT[1], u, NG), bank(3, KEYS, NG * TT).rearrange("p (b q) -> p b q", q=T), S_P, diag(PT[0], u, NG)).then_inc(ptl_done, 1)

            def outputs(t, u):
                dve.wait_ge(o_mm, DONE(t))
                o = bank(7, TT, NG * VC).rearrange("p (g c) -> p g c", g=NG)
                rd = RD[:, u * HEADS:(u + 1) * HEADS].rearrange("p (g h) -> p g h", g=NG)
                dve.wait_ge(yf_done, FREE2(t))
                nc.vector.reciprocal(rd, o[:, :, GC:VC]).then_inc(rd_done, 1)
                dve.wait_ge(rd_done, DONE(t))
                dve.wait_ge(yl_done, FREE2(t))
                nc.vector.tensor_tensor(
                    YF[:, u * C:(u + 1) * C].rearrange("p (g h d) -> p g h d", g=NG, h=GH),
                    o[:, :, 0:GC].rearrange("p g (h d) -> p g h d", h=GH),
                    rd.unsqueeze(3).to_broadcast([TT, NG, GH, HD]), ALU.mult).then_inc(yf_done, 1)

            dve.wait_ge(const_in, 16 * len(CONSTS))
            dve.wait_ge(consts_set, FILLS)
            qkv_lo(0, 0)
            shift(0, 0)
            values(0, 0)
            qkv_lo(1, 1)
            probs_lo(0, 0)
            with dve.Fori(0, (NT - 2) // 2) as i:
                for u in range(2):
                    t = i * 2 + (1 + u)
                    shift(t, 1 - u)
                    outputs(t - 1, u)
                    values(t, 1 - u)
                    qkv_lo(t + 1, u)
                    probs_lo(t, 1 - u)
            shift(NT - 1, 1)
            outputs(NT - 2, 0)
            values(NT - 1, 1)
            probs_lo(NT - 1, 1)
            outputs(NT - 1, 1)

            def residual(t, u):
                dve.wait_ge(op_mm, DONE(t))
                nc.vector.scalar_tensor_tensor(htile(t), bank(2 + u, TT, C), 1 / S_XW, htile(t), ALU.mult, ALU.add).then_inc(h2_done, 1)

            residual(0, 0)
            with dve.Fori(0, (NT - 2) // 2) as i:
                for u in range(2):
                    t = i * 2 + (1 + u)
                    dve.wait_ge(h2_done, DONE(t - 1))
                    residual(t, 1 - u)
                    stats(t - 1, st2_done)
            dve.wait_ge(h2_done, DONE(NT - 2))
            residual(NT - 1, 1)
            stats(NT - 2, st2_done)
            dve.wait_ge(h2_done, DONE(NT - 1))
            stats(NT - 1, st2_done)
            variances(st2_done, mv2_done)
            norm(N2, sd2_done, rs2_done)

            def logits(t, u):
                dve.wait_ge(r_mm, DONE(t))
                nc.vector.tensor_copy(LG[:, ds(t * E, E)], bank(4 + u, TT, E)).then_inc(lg_done, 1)

            norm_row(N2, 1, 1)
            norm_lo(N2, 0, 0)
            with dve.Fori(0, (NT - 2) // 2) as i:
                for u in range(2):
                    t = i * 2 + (1 + u)
                    norm_row(N2, t + 1, u)
                    norm_lo(N2, t, 1 - u)
                    logits(t - 1, u)
            norm_lo(N2, NT - 1, 1)
            logits(NT - 2, 0)
            logits(NT - 1, 1)

            dve.wait_ge(lg_done, DONE(NT - 1))
            dve.wait_ge(pt_mm, DONE(NT - 1))
            dve.wait_ge(w_lo, 2 * PIECES + 2)
            for t in range(NT):
                nc.vector.max(M8[:, t * E:(t + 1) * E], LG[:, t * E:(t + 1) * E]).then_inc(mx_done, 1)
            for t in range(NT):
                dve.wait_ge(mx_done, t + NT + 1 + CR)
                nc.vector.max_index(I8[:, t * E:(t + 1) * E], M8[:, t * E:(t + 1) * E], LG[:, t * E:(t + 1) * E]).then_inc(lg_done, 1)
            dve.wait_ge(lg_done, 2 * NT + CR)
            m8 = M8.rearrange("p (t e) -> p t e", e=E)
            i8 = I8.rearrange("p (t e) -> p t e", e=E)
            col = [RT[:, n * NT:(n + 1) * NT] for n in range(6)]
            nc.vector.tensor_tensor(col[0], m8[:, :, 1], m8[:, :, 0], ALU.subtract).then_inc(route, 1)
            for k in range(2):
                nc.vector.tensor_copy(col[2 + k], i8[:, :, k]).then_inc(route, 1)
            dve.wait_ge(route, 3)
            for k in range(2):
                nc.vector.tensor_tensor(OH[k].rearrange("p (t e) -> p t e", e=E), EID[:, :].unsqueeze(1).to_broadcast([TT, NT, E]),
                                        col[2 + k].unsqueeze(2).to_broadcast([TT, NT, E]), ALU.is_equal).then_inc(route, 1)
            dve.wait_ge(gap_exp, 1)
            nc.vector.tensor_scalar(col[4], col[1], 1.0, S_G * S_W, ALU.add, ALU.mult).then_inc(route, 1)
            dve.wait_ge(route, 6)
            nc.vector.reciprocal(col[4], col[4]).then_inc(route, 1)
            dve.wait_ge(route, 7)
            nc.vector.tensor_tensor(col[5], col[4], col[1], ALU.mult).then_inc(route, 1)
            dve.wait_ge(route, 8)
            for k in range(2):
                oh = OH[k].rearrange("p (t e) -> p t e", e=E)
                nc.vector.tensor_tensor(oh, oh, col[4 + k].unsqueeze(2).to_broadcast([TT, NT, E]), ALU.mult).then_inc(route, 1)
            dve.wait_ge(route, 10)
            nc.vector.tensor_tensor(GW, OH[0], OH[1], ALU.add).then_inc(route, 1)
            dve.wait_ge(route, 11)

            def hidden_lo(n, u):
                dve.wait_ge(gh_done, DONE(n))
                g = slice(u * FC * TT, (u + 1) * FC * TT)
                low(GP[1][:, g], G[:, g], S_G, GP[0][:, g]).then_inc(gl_done, 1)

            def add(e, t, n, u):
                dve.wait_ge(down_mm, DONE(n))
                nc.vector.scalar_tensor_tensor(htile(t), bank(4 + u, TT, C), GW[:, ds(t * E + e, 1)], htile(t), ALU.mult, ALU.add).then_inc(acc_done, 1)

            with dve.Fori(0, E) as e:
                with dve.Fori(0, NT // 2) as i:
                    for u in range(2):
                        hidden_lo(e * NT + (i * 2 + u), u)
                    for u in range(2):
                        add(e, i * 2 + u, e * NT + (i * 2 + u), u)

        @block.tensor
        def _(pe):
            for s in (emb_mm, N1[3], qk_mm, v_mm, s_mm, pt_mm, vr_mm, o_mm, yt_mm, op_mm, N2[3], r_mm, up_mm, down_mm):
                pe.sem_inc(s, CR)

            def embed(t, u):
                pe.wait_ge(xl_done, DONE(t))
                pe.wait_ge(h_done, FREE2(t))
                n = 0
                for k in range(KT):
                    for a, b in PRODUCTS:
                        ins = nc.tensor.matmul(bank(u, TT, C), xhl(u, a)[:, k * TT:(k + 1) * TT], WT[b][:, k * C:(k + 1) * C],
                                               start=n == 0, stop=n == 3 * KT - 1)
                        n += 1
                ins.then_inc(emb_mm, 1)

            pe.wait_ge(small_lo, 1)
            with pe.Fori(0, NT // 2) as i:
                for u in range(2):
                    embed(i * 2 + u, u)

            def norm_transpose(N, t, u):
                pe.wait_ge(N[2], DONE(t))
                pe.wait_ge(N[4], FREE2(t))
                for p in range(2):
                    for c in range(2):
                        n = 2 * p + c
                        ins = nc.tensor.transpose(bank(2 + u, HC, 4 * TT, F16)[:, n * TT:(n + 1) * TT],
                                                  XP[:, u * 2 * C + n * HC:u * 2 * C + (n + 1) * HC], IDH[0:TT, 0:TT])
                ins.then_inc(N[3], 1)

            pe.wait_ge(const_in, 16 * len(CONSTS))
            with pe.Fori(0, NT // 2) as i:
                for u in range(2):
                    norm_transpose(N1, i * 2 + u, u)

            def qkv(t, u):
                pe.wait_ge(N1[4], DONE(t))
                pe.wait_ge(ql_done, FREE1(t))
                pe.wait_ge(kl_done, FREE1(t))
                for j in range(4):
                    n = 0
                    for c in range(2):
                        for a, b in PRODUCTS:
                            ins = nc.tensor.matmul(bank(0, HC, 4 * TT)[:, j * TT:(j + 1) * TT],
                                                   WA[a][:, c * 3 * C + j * HC:c * 3 * C + (j + 1) * HC], xn(t, b, c), start=n == 0, stop=n == 5)
                            n += 1
                ins.then_inc(qk_mm, 1)
                pe.wait_ge(vl_done, FREE1(t))
                n = 0
                for c in range(2):
                    for a, b in PRODUCTS:
                        ins = nc.tensor.matmul(bank(1, TT, C), xn(t, a, c), WA[b][:, c * 3 * C + 2 * C:(c + 1) * 3 * C], start=n == 0, stop=n == 5)
                        n += 1
                ins.then_inc(v_mm, 1)

            def scores(t, u):
                pe.wait_ge(ql_done, DONE(t))
                pe.wait_ge(kbh_done, DONE(t))
                pe.wait_ge(kbl_done, DONE(t))
                pe.wait_ge(sub_done, FREE1(t))
                nc.tensor.matmul(bank(2, TT, HEADS * T), SELQ[:, :], CAUS[:, :].unsqueeze(1).to_broadcast([T, HEADS, T]), start=True, stop=False)
                for c in range(2):
                    for b in range(TI):
                        for p, q in PRODUCTS:
                            at = (2 * u + c) * DW + b * TT
                            keys = kbd(q, u).rearrange("p (c h k) -> p c h k", c=2, h=HH)[:, c, :, b * T:(b + 1) * T]
                            ins = nc.tensor.matmul(bank(2, TT, HEADS * T)[:, c * HH * T:(c + 1) * HH * T], QM[p][:, at:at + TT], keys,
                                                   start=False, stop=(c, b, p) == (1, TI - 1, 1))
                ins.then_inc(s_mm, 1)

            def transpose_probs(t, u):
                pe.wait_ge(p_done, DONE(t))
                pe.wait_ge(ptl_done, FREE1(t))
                for g in range(NG):
                    at = u * HEADS * T + g * KEYS
                    ins = nc.tensor.transpose(bank(3, KEYS, NG * TT)[:, g * TT:(g + 1) * TT], PR[:, at:at + KEYS], IDF[0:TT, 0:TT])
                ins.then_inc(pt_mm, 1)

            def spread_values(t, u):
                pe.wait_ge(vl_done, DONE(t))
                pe.wait_ge(vbl_done, FREE1(t))
                for b in range(TI):
                    for p in range(2):
                        ins = nc.tensor.matmul(bank(4 + b, KEYS, 2 * C)[:, p * C:(p + 1) * C], SELV[:, b * KEYS:(b + 1) * KEYS],
                                               VP[p][:, u * C:(u + 1) * C], start=True, stop=True)
                ins.then_inc(vr_mm, 1)

            def outputs(t, u):
                pe.wait_ge(ptl_done, DONE(t))
                pe.wait_ge(vbl_done, DONE(t))
                pe.wait_ge(yf_done, FREE1(t))
                for g in range(NG):
                    n = 0
                    for b in range(TI):
                        for p, q in PRODUCTS:
                            at = (u * NG + g) * DW + b * TT
                            vat = (b * NG + g) * VC
                            ins = nc.tensor.matmul(bank(7, TT, NG * VC)[:, g * VC:(g + 1) * VC], PT[p][:, at:at + TT],
                                                   vbd(q, u)[:, vat:vat + VC], start=n == 0, stop=n == 3 * TI - 1)
                            n += 1
                ins.then_inc(o_mm, 1)

            pe.wait_ge(small_lo, len(SMALL))
            pe.wait_ge(consts_set, FILLS)
            pe.wait_ge(h_done, DONE(NT - 1))
            pe.wait_ge(N1[4], DONE(NT - 1))
            qkv(0, 0)
            scores(0, 0)
            spread_values(0, 0)
            qkv(1, 1)
            transpose_probs(0, 0)
            with pe.Fori(0, (NT - 2) // 2) as i:
                for u in range(2):
                    t = i * 2 + (1 + u)
                    scores(t, 1 - u)
                    outputs(t - 1, u)
                    spread_values(t, 1 - u)
                    qkv(t + 1, u)
                    transpose_probs(t, 1 - u)
            scores(NT - 1, 1)
            outputs(NT - 2, 0)
            spread_values(NT - 1, 1)
            transpose_probs(NT - 1, 1)
            outputs(NT - 1, 1)

            def transpose_y(t, u):
                pe.wait_ge(yl_done, DONE(t))
                pe.wait_ge(yt_done, FREE2(t))
                for p in range(2):
                    for c in range(2):
                        n = 2 * p + c
                        ins = nc.tensor.transpose(bank(u, HC, 4 * TT, F16)[:, n * TT:(n + 1) * TT], Y[p][:, ds(t * C + c * HC, HC)], IDH[0:TT, 0:TT])
                ins.then_inc(yt_mm, 1)

            def project(t, u):
                pe.wait_ge(yt_done, DONE(t))
                pe.wait_ge(h2_done, FREE2(t))
                n = 0
                for c in range(2):
                    for a, b in PRODUCTS:
                        at = u * 4 * TT + (2 * a + c) * TT
                        ins = nc.tensor.matmul(bank(2 + u, TT, C), YT[:, at:at + TT], WO[b][:, c * C:(c + 1) * C], start=n == 0, stop=n == 5)
                        n += 1
                ins.then_inc(op_mm, 1)

            pe.wait_ge(ptl_done, DONE(NT - 1))
            pe.wait_ge(vl_done, DONE(NT - 1))
            transpose_y(0, 0)
            with pe.Fori(0, (NT - 2) // 2) as i:
                for u in range(2):
                    transpose_y(i * 2 + (u + 1), 1 - u)
                    project(i * 2 + u, u)
            transpose_y(NT - 1, 1)
            project(NT - 2, 0)
            project(NT - 1, 1)

            def router(t, u):
                pe.wait_ge(N2[4], DONE(t))
                pe.wait_ge(lg_done, FREE2(t))
                n = 0
                for c in range(2):
                    for a, b in PRODUCTS:
                        ins = nc.tensor.matmul(bank(4 + u, TT, E), xn(t, a, c)[0:HC], WR[b][:, c * E:(c + 1) * E], start=n == 0, stop=n == 5)
                        n += 1
                ins.then_inc(r_mm, 1)

            pe.wait_ge(h2_done, DONE(NT - 1))
            norm_transpose(N2, 0, 0)
            with pe.Fori(0, (NT - 2) // 2) as i:
                for u in range(2):
                    norm_transpose(N2, i * 2 + (u + 1), 1 - u)
                    router(i * 2 + u, u)
            norm_transpose(N2, NT - 1, 1)
            router(NT - 2, 0)
            router(NT - 1, 1)

            def up(e, t, n, u):
                pe.wait_ge(gelu_done, FREE2(n))
                for f in range(FC):
                    w = f % (FC // 2) * TT
                    k = 0
                    for c in range(2):
                        for a, b in PRODUCTS:
                            ins = nc.tensor.matmul(bank(2 * u + f // (FC // 2), 128, FC // 2 * TT)[:, w:w + TT],
                                                   W1[a][:, ds(e * 2 * F + (c * F + f * 128), 128)], xn(t, b, c), start=k == 0, stop=k == 5)
                            k += 1
                ins.then_inc(up_mm, 1)

            def down(e, n, u):
                pe.wait_ge(gl_done, DONE(n))
                pe.wait_ge(acc_done, FREE2(n))
                for f in range(FC):
                    for a, b in PRODUCTS:
                        at = (u * FC + f) * TT
                        ins = nc.tensor.matmul(bank(4 + u, TT, C), GP[a][:, at:at + TT], W2[b][:, ds(e * FC * C + f * C, C)],
                                               start=(f, a, b) == (0, 0, 0), stop=False)
                for p in range(2):
                    ins = nc.tensor.matmul(bank(4 + u, TT, C), ONE[:, 0:TT], B2[p][:, ds(e * C, C)], start=False, stop=p == 1)
                ins.then_inc(down_mm, 1)

            pe.wait_ge(w_lo, 2 * PIECES + 2)
            pe.wait_ge(lg_done, DONE(NT - 1))
            with pe.Fori(0, E) as e:
                with pe.Fori(0, NT // 2) as i:
                    for u in range(2):
                        up(e, i * 2 + u, e * NT + (i * 2 + u), u)
                    for u in range(2):
                        down(e, e * NT + (i * 2 + u), u)


def kernel(**inputs):
    import ml_dtypes
    import concourse.bacc as bacc
    from concourse.bass_utils import run_bass_kernel_spmd

    def arr(name):
        return np.asarray(inputs[name])

    def ones_row(w, bias):
        cols = w.shape[1]
        r = np.zeros((HC + 1, 2, cols), w.dtype)
        r[0:HC] = w.reshape(2, HC, cols).transpose(1, 0, 2)
        r[HC, 1] = bias
        return r.reshape(HC + 1, 2 * cols)

    x = arr("x").reshape(B, CIN, SIDE, PATCH, SIDE, PATCH).transpose(0, 2, 4, 3, 5, 1).reshape(B * T, DTOK)
    xp = np.zeros((NT * TT, DTOK), x.dtype)
    xp[0:B * T] = x
    w1 = arr("L0_ffn_w1")
    w1p = np.stack([ones_row(w1[e], arr("L0_ffn_b1")[e]) for e in range(E)], 1)
    key = np.arange(KEYS)
    ch = np.arange(C)
    tok = np.arange(TT)
    data = {
        "xt": xp.reshape(NT, TT, KT, 128).transpose(0, 3, 2, 1).reshape(NT, 128, KT * TT),
        "wtok": arr("L0_tok_W").reshape(KT, 128, C).transpose(1, 0, 2).reshape(128, KT * C),
        "wqkv": ones_row(arr("L0_attn_W_attn").T, arr("L0_attn_b_attn")),
        "wo": ones_row(arr("L0_attn_W_o").T, arr("L0_attn_b_o")),
        "wr": arr("L0_ffn_router_w").T.reshape(2, HC, E).transpose(1, 0, 2).reshape(HC, 2 * E),
        "w1": w1p.reshape(HC + 1, E * 2 * F),
        "w2": arr("L0_ffn_w2").reshape(E, FC, 128, C).transpose(2, 0, 1, 3).reshape(128, E * FC * C),
        "b2": arr("L0_ffn_b2").reshape(1, E * C),
        "idf": np.eye(128, dtype=np.float32),
        "idh": np.eye(128, dtype=np.float16),
        "selq": (np.arange(T)[:, None] == tok[None, :] % T).astype(ml_dtypes.bfloat16),
        "causal": np.where(np.arange(T)[:, None] >= np.arange(T)[None, :], 0.0, -1e30).astype(ml_dtypes.bfloat16),
        "selv": np.stack([tok[:, None] == b * T + key[None, :] % T for b in range(TI)], 1).reshape(TT, TI * KEYS).astype(np.float16),
        "hmask": np.repeat(np.arange(HC)[:, None] // HD == np.arange(HH)[None, :], TT, 1).astype(np.float16),
        "vmask": (key[:, None] // T == ch[None, :] // HD % GH).astype(np.float32),
        "vones": (key[:, None] // T == np.arange(GH)[None, :]).astype(np.float16),
        "eid": np.tile(np.arange(E), (TT, 1)).astype(np.float32),
    }
    nc = bacc.Bacc("TRN2", target_bir_lowering=False, num_devices=1)
    arrays, args = {}, []
    for name, a in data.items():
        arrays[name] = np.ascontiguousarray(a)
        args.append(nc.dram_tensor(name, a.shape, mybir.dt.from_np(a.dtype), kind="ExternalInput").ap())
    args.append(nc.dram_tensor("out", (B, T, C), F32, kind="ExternalOutput").ap())
    build(nc, *args)
    r = run_bass_kernel_spmd(nc, [arrays], core_ids=[0])
    return r.results[0]["out"]
```

```python
from contextlib import ExitStack

import numpy as np
import concourse.bass as bass
from concourse import mybir

F32 = mybir.dt.float32
F16 = mybir.dt.float16
BF16 = mybir.dt.bfloat16
U32 = mybir.dt.uint32
ALU = mybir.AluOpType
ACT = mybir.ActivationFunctionType
AX = mybir.AxisListType

B, CIN, IMG, PATCH = 64, 3, 96, 16
SIDE = IMG // PATCH
T = SIDE * SIDE
C, HEADS = 192, 12
HD = C // HEADS
E, F = 8, 768
DTOK = CIN * PATCH * PATCH
KT = DTOK // 128

TI = 3
TT = TI * T
NT = -(-B // TI)
HC = C // 2
HH = HEADS // 2
GH = 3
NG = HEADS // GH
KEYS = GH * T
GC = GH * HD
VC = GC + GH
FC = F // 128
LAST = B * T - (NT - 1) * TT

TOPK = 2
ST_ = 128
NS = TOPK * B * T // ST_ + E - 1
ROW = C + 4
TOKEN, FIRST, GAP, SECOND = range(C, ROW)
DUMP = ST_

S_X, S_W = 2.0 ** 8, 2.0 ** 10
S_XW = S_X * S_W
S_Q, S_V, S_P, S_G = 2.0 ** 6, 2.0 ** 8, 2.0 ** 12, 2.0 ** 6
EPS = 1e-5
PRODUCTS = [(0, 0), (0, 1), (1, 0)]

CR = 2


def DONE(t):
    return t + 1 + CR


def FREE2(t):
    return t + 1


def ADDED(n):
    return 16 * n


def FREE1(t):
    return t + CR


def build(nc, xt, wtok, wqkv, wo, wr, w1, w2, idf, idh, selq, causal, selv, hmask, vmask, vones, eid,
          before, tileno, tokens, real, empty, slots, out):
    ds = bass.ds
    ctx = ExitStack()
    with ctx:
        def sb(name, shape, dt=F32):
            return ctx.enter_context(nc.sbuf_tensor(name, shape, dt))

        def sem(name):
            return ctx.enter_context(nc.semaphore(name))

        H = sb("H", [TT, NT * C])
        XN = sb("XN", [HC + 1, NT * 4 * TT], F16)
        W1 = [sb(f"W1{p}", [HC + 1, E * 2 * F], F16) for p in "hl"]
        W2E = FC * C + C
        W2 = [sb(f"W2{p}", [128, E * W2E], F16) for p in "hl"]
        ST = sb("ST", [TT, NT * 6])
        MEAN = sb("MEAN", [TT, NT])
        VAR = sb("VAR", [TT, NT])
        DM = sb("DM", [TT, NT])
        SCALE = sb("SCALE", [128, 1])
        RS = sb("RS", [TT, NT])
        EPSV = sb("EPSV", [TT, 1])
        ONE = sb("ONE", [1, 128], F16)
        IDF = sb("IDF", [128, 128])
        IDH = sb("IDH", [128, 128], F16)
        SELQ = sb("SELQ", [T, TT], BF16)
        CAUS = sb("CAUS", [T, T], BF16)
        SELV = sb("SELV", [TT, TI * KEYS], F16)
        HM = sb("HM", [HC, HH * TT], F16)
        VM = sb("VM", [KEYS, C])
        VO = sb("VO", [KEYS, GH], F16)
        EID = sb("EID", [TT, E])
        WA = [sb(f"WA{p}", [HC + 1, 2 * 3 * C], F16) for p in "hl"]
        WO = [sb(f"WO{p}", [HC + 1, 2 * C], F16) for p in "hl"]
        WR = [sb(f"WR{p}", [HC, 2 * E], F16) for p in "hl"]
        WSTG = sb("WSTG", [128, 2 * F])
        REG = sb("REG", [128, max(6 * KT * TT, NT * ROW)])
        XW = KT * TT
        XHL = REG[:, 4 * XW:6 * XW].bitcast(F16)
        Y = [REG[0:TT, p * NT * C // 2:(p + 1) * NT * C // 2].bitcast(F16) for p in range(2)]
        RB = REG[0:TT, 0:NT * ROW]
        RBH = RB.bitcast(F16)
        KW = 2 * HH * TT
        KBR = sb("KBR", [128, 2 * KW])
        KB = [KBR[0:HC, p * KW:(p + 1) * KW].bitcast(F16) for p in range(2)]
        WT = [KBR[:, p * KT * C // 2:(p + 1) * KT * C // 2].bitcast(F16) for p in range(2)]
        cut = [0]

        def after(cols):
            cut[0] += cols
            return KBR[:, cut[0] - cols:cut[0]]

        XR = [after(C) for _ in range(2)]
        XM = [after(ROW - C) for _ in range(2)]
        YO = [after(C) for _ in range(2)]
        IDX = [after(1).bitcast(U32) for _ in range(2)]
        MATCH = [after(1) for _ in range(2)]
        GATE = [after(1) for _ in range(2)]
        BEFORE = after(64).bitcast(F16)[0:TT]
        ONES = after(64).bitcast(F16)[0:TT]
        TILENO, TOKENS, REAL = after(NS), after(NT)[0:TT], after(1)[0:TT]
        EXPF, EXPI = after(NS), after(NS).bitcast(mybir.dt.int32)
        PASSED = after(NS * (E - 1))
        CNTI = after(E).bitcast(mybir.dt.int32)
        CUM = [after(2 * E) for _ in range(2)]
        START = after(E)
        JUNK, JUNK2 = after(1), after(1)[0:1]
        DW = TI * (TT + T)
        PTR = sb("PTR", [128, 2 * NG * DW])
        PT = [PTR[0:KEYS, p * NG * DW:(p + 1) * NG * DW].bitcast(F16) for p in range(2)]
        SMALL = [(wtok, WT, 128, KT * C), (wqkv, WA, HC + 1, 6 * C), (wo, WO, HC + 1, 2 * C), (wr, WR, HC, 2 * E)]
        RAW, at = [], 0
        for _, _, rows, cols in SMALL:
            RAW.append(PTR[0:rows, at:at + cols])
            at += cols
        G = PTR[:, 0:2 * F]
        GP = [PTR[:, (2 + p) * F:(3 + p) * F].bitcast(F16) for p in range(2)]
        XF = sb("XF", [TT, 2 * C])
        XP = sb("XP", [TT, 2 * 2 * C], F16)
        QM = [sb(f"QM{p}", [HC, 2 * 2 * DW], F16) for p in "hl"]
        KP = [sb(f"KP{p}", [HC, 2 * 2 * TT], F16) for p in "hl"]
        VP = [sb(f"VP{p}", [TT, 2 * C], F16) for p in "hl"]
        VB = [sb(f"VB{p}", [KEYS, 2 * TI * NG * VC], F16) for p in "hl"]
        LG = VB[0][:, 0:2 * NT * E].bitcast(F32)
        MX = sb("MX", [TT, 2 * HEADS])
        PR = sb("PR", [TT, 2 * HEADS * T])
        RD = sb("RD", [TT, 2 * HEADS])
        YF = sb("YF", [TT, 2 * C])
        YT = sb("YT", [HC + 1, 2 * 4 * ST_], F16)
        M8 = PR[:, 0:NT * E]
        I8 = PR[:, NT * E:2 * NT * E].bitcast(U32)
        OH = [WSTG[0:TT, n * NT * E:(n + 1) * NT * E] for n in range(2)]
        OWN = [WSTG[0:TT, (2 + n) * NT * E:(3 + n) * NT * E] for n in range(2)]
        SLOTS = WSTG[0:TT, 4 * NT * E:5 * NT * E]
        CHOSEN = WSTG[0:TT, 5 * NT * E:5 * NT * E + NT * E // 2].bitcast(F16)
        RT = PR[:, 2 * NT * E:2 * NT * E + 8 * NT]
        SLOTI = PR[:, 2 * NT * E + 8 * NT:2 * NT * E + 10 * NT].bitcast(U32)

        PSA = ctx.enter_context(nc.psum_tensor("PSA", [128, 8 * 512], F32))

        def bank(n, rows, cols, dt=F32):
            v = PSA[0:rows, n * 512:(n + 1) * 512]
            return (v.bitcast(dt) if dt != F32 else v)[:, 0:cols]

        const_in, consts_set = sem("const_in"), sem("consts_set")
        raw_in = [sem(f"raw_in{n}") for n in range(4)]
        small_hi, small_lo = sem("small_hi"), sem("small_lo")
        pt_zero = sem("pt_zero")
        x_in = [sem(f"x_in{n}") for n in range(2)]
        xh_done, xl_done, emb_mm, h_done = [sem(n) for n in ("xh_done", "xl_done", "emb_mm", "h_done")]
        st_done, mv_done, sd_done, rs_done = [sem(n) for n in ("st_done", "mv_done", "sd_done", "rs_done")]
        N1 = [sem(f"norm1_{n}") for n in ("row", "hi", "lo", "transposed", "done")]
        qk_mm, v_mm = sem("qk_mm"), sem("v_mm")
        qh_done, kh_done, vh_done = sem("qh_done"), sem("kh_done"), sem("vh_done")
        ql_done, kl_done, vl_done = sem("ql_done"), sem("kl_done"), sem("vl_done")
        kbh_done, kbl_done = sem("kbh_done"), sem("kbl_done")
        s_mm, mx_done, sub_done, p_done = sem("s_mm"), sem("mx_done"), sem("sub_done"), sem("p_done")
        pt_mm, pth_done, ptl_done = sem("pt_mm"), sem("pth_done"), sem("ptl_done")
        vr_mm, vbh_done, vbl_done = sem("vr_mm"), sem("vbh_done"), sem("vbl_done")
        o_mm, rd_done, yf_done, yh_done, yl_done = [sem(n) for n in ("o_mm", "rd_done", "yf_done", "yh_done", "yl_done")]
        yt_mm, yt_done, op_mm, h2_done, st2_done, mv2_done = [sem(n) for n in ("yt_mm", "yt_done", "op_mm", "h2_done", "st2_done", "mv2_done")]
        sd2_done, rs2_done = sem("sd2_done"), sem("rs2_done")
        N2 = [sem(f"norm2_{n}") for n in ("row", "hi", "lo", "transposed", "done")]
        r_mm, lg_done = sem("r_mm"), sem("lg_done")
        route, gap_exp = sem("route"), sem("gap_exp")
        b2_in = sem("b2_in")
        w_in = [sem(f"w_in{n}") for n in range(2)]
        w_scaled, w_hi, w_lo = sem("w_scaled"), sem("w_hi"), sem("w_lo")
        later_in, ones_set, empty_in, h_stored = sem("later_in"), sem("ones_set"), sem("empty_in"), sem("h_stored")
        rank_mm, count, dispatched = sem("rank_mm"), sem("count"), sem("dispatched")
        rows_in = [sem(f"rows_in{n}") for n in range(2)]
        meta_in = [sem(f"meta_in{n}") for n in range(2)]
        match_done, gate_done, xr_mm, xt_done = sem("match_done"), sem("gate_done"), sem("xr_mm"), sem("xt_done")
        up_mm, gelu_done, gh_done, gl_done, down_mm, y_done = [sem(n) for n in ("up_mm", "gelu_done", "gh_done", "gl_done", "down_mm", "y_done")]
        y_added, add_turn = sem("y_added"), sem("add_turn")
        CONSTS = [(IDF, idf), (IDH, idh), (SELQ, selq), (CAUS, causal), (SELV, selv), (HM, hmask), (VM, vmask), (VO, vones), (EID, eid)]
        LATER = [(BEFORE, before), (TILENO, tileno), (TOKENS, tokens), (REAL, real)]
        ROUTED = 15
        FILLS = 12
        block = ctx.enter_context(nc.Block())

        def xs(slot, k):
            return REG[:, (2 * slot + k) * XW:(2 * slot + k + 1) * XW]

        def xhl(u, p):
            return XHL[:, (2 * u + p) * XW:(2 * u + p + 1) * XW]

        def htile(t):
            return H[:, ds(t * C, C)]

        def xn(t, p, c):
            return XN[:, ds(t * (4 * TT) + (2 * p + c) * TT, TT)]

        def diag(buf, u, n):
            return buf[:, u * n * DW:(u + 1) * n * DW].rearrange("p (b q) -> p b q", q=TT + T)[:, :, 0:T]

        def kbd(p, u):
            return KB[p][:, u * KW:(u + 1) * KW]

        def vbd(p, u):
            return VB[p][:, u * TI * NG * VC:(u + 1) * TI * NG * VC]

        def heads(ap):
            return ap.rearrange("p (h k) -> p h k", h=HEADS)

        def row_part(N, t, u, at, cols):
            return XP[:, u * 2 * C + at:u * 2 * C + at + cols] if N is N1 else RBH[:, ds(t * (2 * ROW) + at, cols)]

        PIECES = 2 * E

        @block.sync
        def _(sp):
            def patches(pair, slot):
                sp.dma_start(REG[:, slot * 2 * XW:(slot + 1) * 2 * XW].rearrange("p (t c) -> p t c", t=2),
                             xt[ds(pair * 2, 2), :, :].rearrange("t p c -> p t c")).then_inc(x_in[slot], 16)

            sp.dma_start(RAW[0], wtok).then_inc(raw_in[0], 16)
            patches(0, 0)
            patches(1, 1)
            for n in range(1, len(SMALL)):
                sp.dma_start(RAW[n], SMALL[n][0]).then_inc(raw_in[n], 16)
            for dst, src in CONSTS:
                sp.dma_start(dst[:, :], src).then_inc(const_in, 16)
            LOOPED = (NT // 2 - 3) // 2
            with sp.Fori(0, LOOPED) as i:
                for slot in range(2):
                    sp.wait_ge(xl_done, i * 4 + (2 * slot + 2 + CR))
                    patches(i * 2 + (2 + slot), slot)
            for pair in range(2 + 2 * LOOPED, NT // 2):
                sp.wait_ge(xl_done, 2 * (pair - 1) + CR)
                patches(pair, pair % 2)
            with sp.Fori(0, PIECES // 2) as i:
                for u in range(2):
                    sp.wait_ge(w_lo, i * 2 + (u + 1))
                    sp.dma_start(WSTG[0:HC + 1, u * F:(u + 1) * F], w1[:, ds((i * 2 + u) * F, F)]).then_inc(w_in[u], 16)
            with sp.Fori(0, PIECES // 2) as i:
                for u in range(2):
                    sp.wait_ge(w_lo, i * 2 + (PIECES + u + 1))
                    sp.dma_start(WSTG[:, u * F:u * F + W2E // 2], w2[:, ds((i * 2 + u) * (W2E // 2), W2E // 2)]).then_inc(w_in[u], 16)
            sp.dma_start(slots.rearrange("(n p) c -> p n c", p=ST_), empty.unsqueeze(1).to_broadcast([ST_, NS, ROW])).then_inc(empty_in, 16)
            sp.wait_ge(h2_done, DONE(NT - 1))
            sp.dma_start(out[0:(NT - 1) * TT, :].rearrange("(t p) c -> p t c", p=TT),
                         H[:, 0:(NT - 1) * C].rearrange("p (t c) -> p t c", c=C)).then_inc(h_stored, 16)
            sp.dma_start(out[(NT - 1) * TT:B * T, :], H[0:LAST, (NT - 1) * C:NT * C]).then_inc(h_stored, 16)
            sp.dma_start(out[B * T:B * T + DUMP, :], empty[:, 0:C]).then_inc(h_stored, 16)
            sp.wait_ge(s_mm, DONE(NT - 1))
            for dst, src in LATER:
                sp.dma_start(dst, src).then_inc(later_in, 16)
            sp.wait_ge(dispatched, 16 * TOPK * NT)
            sp.wait_ge(empty_in, 16)

            def load_rows(s, u, free):
                at = ds(s * ST_, ST_)
                if free:
                    sp.wait_ge(xr_mm, FREE2(s))
                sp.dma_start(XR[u], slots[at, 0:C]).then_inc(rows_in[u], 16)
                if free:
                    sp.wait_ge(gate_done, FREE2(s))
                sp.dma_start(XM[u], slots[at, C:ROW]).then_inc(meta_in[u], 16)

            load_rows(0, 0, False)
            load_rows(1, 1, False)
            with sp.Fori(0, (NS - 3) // 2) as i:
                for u in range(2):
                    load_rows(i * 2 + (2 + u), u, True)
            load_rows(NS - 1, 0, True)
            sp.wait_ge(h_stored, 48)
            sp.wait_ge(y_added, ADDED(NS))

        @block.gpsimd
        def _(gp):
            for s in (kbl_done, yl_done):
                gp.sem_inc(s, CR)
            fills = [(EPSV[:, :], EPS / S_X ** 2), (ONE[:, :], S_G), (SCALE[:, :], S_W), (XN[HC:HC + 1, :], 0.0),
                     (XN[HC:HC + 1, :].rearrange("p (t c) -> p t c", t=NT)[:, :, 0:2 * TT], S_X),
                     (YT[HC:HC + 1, :], 0.0), (YT[HC:HC + 1, :].rearrange("p (t c) -> p t c", t=2)[:, :, 0:2 * ST_], S_X)]
            fills += [(buf[p][:, :], 0.0) for buf in (QM, VB) for p in range(2)]
            for n, (dst, value) in enumerate(fills):
                if n:
                    gp.wait_ge(consts_set, n)
                nc.gpsimd.memset(dst, value).then_inc(consts_set, 1)
            gp.wait_ge(consts_set, len(fills))
            gp.wait_ge(const_in, 16 * len(CONSTS))
            nc.gpsimd.tensor_copy(VB[0][:, :].rearrange("p (n c) -> p n c", c=VC)[:, :, GC:VC],
                                  VO[:, :].unsqueeze(1).to_broadcast([KEYS, 2 * TI * NG, GH])).then_inc(consts_set, 1)
            gp.wait_ge(consts_set, FILLS)
            gp.wait_ge(small_lo, len(SMALL))
            nc.gpsimd.memset(PTR[:, :], 0.0).then_inc(pt_zero, 1)

            def split_w(n, raw, parts):
                nc.gpsimd.tensor_tensor(raw, raw, SCALE[0:raw.shape[0], 0:1].to_broadcast([raw.shape[0], raw.shape[1]]),
                                        ALU.mult).then_inc(w_scaled, 1)
                gp.wait_ge(w_scaled, n + 1)
                nc.gpsimd.tensor_copy(parts[0], raw).then_inc(w_hi, 1)
                gp.wait_ge(w_hi, n + 1)
                nc.gpsimd.tensor_tensor(parts[1], raw, parts[0], ALU.subtract).then_inc(w_lo, 1)

            gp.sem_inc(w_lo, 2)

            def w1_piece(i, u):
                gp.wait_ge(w_in[u], i * 16 + 16)
                at = (i * 2 + u) * F
                split_w(i * 2 + u, WSTG[0:HC + 1, u * F:(u + 1) * F], [W1[p][:, ds(at, F)] for p in range(2)])

            def w2_piece(i, u):
                gp.wait_ge(w_in[u], i * 16 + (16 + 16 * E))
                w = W2E // 2
                at = (i * 2 + u) * w
                split_w(i * 2 + (u + PIECES), WSTG[:, u * F:u * F + w], [W2[p][:, ds(at, w)] for p in range(2)])

            def keys_low(t, u):
                gp.wait_ge(kl_done, DONE(t))
                gp.wait_ge(s_mm, FREE2(t))
                nc.gpsimd.tensor_tensor(
                    kbd(1, u).rearrange("p (c h k) -> p c h k", c=2, h=HH),
                    KP[1][:, u * 2 * TT:(u + 1) * 2 * TT].rearrange("p (c k) -> p c k", c=2).unsqueeze(2).to_broadcast([HC, 2, HH, TT]),
                    HM[:, :].rearrange("p (h k) -> p h k", h=HH).unsqueeze(1).to_broadcast([HC, 2, HH, TT]),
                    ALU.mult).then_inc(kbl_done, 1)

            def y_parts(t, u):
                gp.wait_ge(yf_done, DONE(t))
                yf = YF[:, u * C:(u + 1) * C]
                nc.gpsimd.tensor_copy(Y[0][:, ds(t * C, C)], yf).then_inc(yh_done, 1)
                gp.wait_ge(yh_done, t + 1)
                nc.gpsimd.tensor_tensor(Y[1][:, ds(t * C, C)], yf, Y[0][:, ds(t * C, C)], ALU.subtract).then_inc(yl_done, 1)

            with gp.Fori(0, PIECES // 2) as i:
                for u in range(2):
                    w1_piece(i, u)
            keys_low(0, 0)
            keys_low(1, 1)
            with gp.Fori(0, (NT - 2) // 2) as i:
                for u in range(2):
                    t = i * 2 + (1 + u)
                    y_parts(t - 1, u)
                    keys_low(t + 1, u)
            y_parts(NT - 2, 0)
            y_parts(NT - 1, 1)
            with gp.Fori(0, PIECES // 2) as i:
                for u in range(2):
                    w2_piece(i, u)
            gp.wait_ge(s_mm, DONE(NT - 1))
            nc.gpsimd.memset(ONES, 1.0).then_inc(ones_set, 1)
            gp.wait_ge(ones_set, 1)
            nc.gpsimd.memset(CUM[0], 0.0).then_inc(ones_set, 1)
            gp.wait_ge(ones_set, 2)
            nc.gpsimd.memset(CUM[1], 0.0).then_inc(ones_set, 1)
            gp.wait_ge(empty_in, 16)
            gp.wait_ge(route, ROUTED)
            for t in range(NT):
                n = TT if t < NT - 1 else LAST
                for k in range(TOPK):
                    gp.indirect_dma_start(out=slots, out_offset=bass.IndirectOffsetOnAxis(ap=SLOTI[0:n, k * NT + t:k * NT + t + 1], axis=0),
                                          in_=RB[0:n, t * ROW:(t + 1) * ROW], in_offset=None).then_inc(dispatched, 16)
            gp.wait_ge(h_stored, 48)

            def add_rows(s, u, first=False):
                if not first:
                    gp.wait_ge(add_turn, s)
                    gp.wait_ge(y_added, ADDED(s))
                gp.wait_ge(y_done, DONE(s))
                nc.gpsimd.tensor_tensor(JUNK[0:1, :], CUM[0][0:1, 0:1], CUM[0][0:1, 0:1], ALU.add).then_inc(add_turn, 1)
                gp.indirect_dma_start(out=out, out_offset=bass.IndirectOffsetOnAxis(ap=IDX[u], axis=0),
                                      in_=YO[u], in_offset=None, compute_op=ALU.add).then_inc(y_added, 16)

            add_rows(0, 0, True)
            with gp.Fori(0, (NS - 1) // 2) as i:
                for v in (1, 2):
                    add_rows(i * 2 + v, v % 2)

        @block.scalar
        def _(act):
            for s in (xh_done, h_done, N1[1], N1[4], qh_done, kh_done, vh_done, p_done, pth_done, yt_done, N2[1], N2[4], gelu_done, gh_done):
                act.sem_inc(s, CR)
            for n, (_, parts, _, _) in enumerate(SMALL):
                act.wait_ge(raw_in[n], 16)
                nc.scalar.activation(parts[0][:, :], RAW[n], ACT.Copy, scale=S_W).then_inc(small_hi, 1)

            def patch_hi(t, u, slot, k, landed):
                act.wait_ge(x_in[slot], landed)
                act.wait_ge(emb_mm, FREE2(t))
                nc.scalar.activation(xhl(u, 0), xs(slot, k), ACT.Copy, scale=S_X).then_inc(xh_done, 1)

            def h_out(t, u):
                act.wait_ge(emb_mm, DONE(t))
                nc.scalar.activation(htile(t), bank(u, TT, C), ACT.Copy, scale=1 / S_XW).then_inc(h_done, 1)

            patch_hi(0, 0, 0, 0, 16)
            with act.Fori(0, (NT - 2) // 4) as i:
                for v in range(4):
                    t, ahead = i * 4 + v, v + 1
                    patch_hi(t + 1, ahead % 2, ahead // 2 % 2, ahead % 2, i * 16 + (16 if ahead < 4 else 32))
                    h_out(t, v % 2)
            patch_hi(NT - 1, 1, 0, 1, 16 * (NT // 4 + 1))
            h_out(NT - 2, 0)
            h_out(NT - 1, 1)

            def deviation(mv, done):
                act.wait_ge(mv, 6)
                nc.scalar.activation(RS[:, :], VAR[:, :], ACT.Sqrt, bias=EPSV[:, 0:1], scale=1 / (C * S_X ** 2)).then_inc(done, 1)

            def norm_hi(N, t, u):
                act.wait_ge(N[0], DONE(t))
                act.wait_ge(N[3], FREE2(t))
                nc.scalar.activation(row_part(N, t, u, 0, C), XF[:, u * C:(u + 1) * C], ACT.Copy).then_inc(N[1], 1)

            def norm_out(N, t, u):
                act.wait_ge(N[3], DONE(t))
                nc.scalar.activation(XN[0:HC, ds(t * (4 * TT), 4 * TT)], bank(2 + u, HC, 4 * TT, F16), ACT.Copy).then_inc(N[4], 1)

            def norm(N):
                norm_hi(N, 0, 0)
                with act.Fori(0, (NT - 2) // 2) as i:
                    for u in range(2):
                        norm_hi(N, i * 2 + (u + 1), 1 - u)
                        norm_out(N, i * 2 + u, u)
                norm_hi(N, NT - 1, 1)
                norm_out(N, NT - 2, 0)
                norm_out(N, NT - 1, 1)

            act.wait_ge(consts_set, 1)
            deviation(mv_done, sd_done)
            norm(N1)

            def qkv_hi(t, u):
                act.wait_ge(qk_mm, DONE(t))
                act.wait_ge(s_mm, FREE2(t))
                qk = bank(0, HC, 4 * TT)
                nc.scalar.activation(diag(QM[0], u, 2), qk[:, 0:2 * TT].rearrange("p (b q) -> p b q", q=T), ACT.Copy,
                                     scale=S_Q / S_XW).then_inc(qh_done, 1)
                act.wait_ge(kbh_done, FREE2(t))
                act.wait_ge(kbl_done, FREE2(t))
                nc.scalar.activation(KP[0][:, u * 2 * TT:(u + 1) * 2 * TT], qk[:, 2 * TT:4 * TT], ACT.Copy,
                                     scale=S_Q / S_XW).then_inc(kh_done, 1)
                act.wait_ge(v_mm, DONE(t))
                act.wait_ge(vr_mm, FREE2(t))
                nc.scalar.activation(VP[0][:, u * C:(u + 1) * C], bank(1, TT, C), ACT.Copy, scale=S_V / S_XW).then_inc(vh_done, 1)

            def exps(t, u):
                act.wait_ge(sub_done, DONE(t))
                pr = PR[:, u * HEADS * T:(u + 1) * HEADS * T]
                nc.scalar.activation(pr, pr, ACT.Exp, scale=HD ** -0.5 / S_Q ** 2).then_inc(p_done, 1)

            def probs_hi(t, u):
                act.wait_ge(pt_mm, DONE(t))
                act.wait_ge(o_mm, FREE2(t))
                nc.scalar.activation(diag(PT[0], u, NG), bank(3, KEYS, NG * TT).rearrange("p (b q) -> p b q", q=T), ACT.Copy,
                                     scale=S_P).then_inc(pth_done, 1)

            act.wait_ge(consts_set, FILLS)
            act.wait_ge(pt_zero, 1)
            qkv_hi(0, 0)
            exps(0, 0)
            qkv_hi(1, 1)
            probs_hi(0, 0)
            with act.Fori(0, (NT - 2) // 2) as i:
                for u in range(2):
                    t = i * 2 + (1 + u)
                    exps(t, 1 - u)
                    qkv_hi(t + 1, u)
                    probs_hi(t, 1 - u)
            exps(NT - 1, 1)
            probs_hi(NT - 1, 1)

            act.wait_ge(consts_set, FILLS)
            with act.Fori(0, NT // 2) as i:
                for u in range(2):
                    t = i * 2 + u
                    act.wait_ge(yt_mm, DONE(t))
                    act.wait_ge(op_mm, FREE2(t))
                    nc.scalar.activation(YT[0:HC, u * 4 * ST_:(u + 1) * 4 * ST_].rearrange("p (n q) -> p n q", q=ST_)[:, :, 0:TT],
                                         bank(u, HC, 4 * TT, F16).rearrange("p (n q) -> p n q", q=TT), ACT.Copy).then_inc(yt_done, 1)
            deviation(mv2_done, sd2_done)
            norm(N2)
            act.wait_ge(route, 3)
            nc.scalar.activation(RT[:, NT:2 * NT], RT[:, 0:NT], ACT.Exp, scale=1 / S_XW).then_inc(gap_exp, 1)
            nc.scalar.activation(JUNK2, EPSV[0:1, :], ACT.Gelu).then_inc(gap_exp, 1)

            def hidden(s, u):
                g = G[:, u * F:(u + 1) * F]
                act.wait_ge(up_mm, DONE(s))
                act.wait_ge(gl_done, FREE2(s))
                nc.scalar.activation(g.rearrange("p (h c) -> p h c", h=2),
                                     PSA[:, 2 * u * 512:(2 * u + 2) * 512].rearrange("p (h c) -> p h c", h=2)[:, :, 0:F // 2],
                                     ACT.Gelu, scale=1 / S_XW).then_inc(gelu_done, 1)
                act.wait_ge(gelu_done, DONE(s))
                act.wait_ge(down_mm, FREE2(s))
                nc.scalar.activation(GP[0][:, u * F:(u + 1) * F], g, ACT.Copy, scale=S_G).then_inc(gh_done, 1)

            with act.Fori(0, (NS - 1) // 2) as i:
                for u in range(2):
                    hidden(i * 2 + u, u)
            hidden(NS - 1, 0)

        @block.vector
        def _(dve):
            for s in (xl_done, st_done, N1[0], N1[2], ql_done, kl_done, vl_done, kbh_done, mx_done, sub_done,
                      ptl_done, vbl_done, rd_done, yf_done, h2_done, st2_done, N2[0], N2[2], lg_done, gl_done, gate_done, xt_done, y_done):
                dve.sem_inc(s, CR)

            def low(dst, src, scale, hi):
                return nc.vector.scalar_tensor_tensor(dst, src, scale, hi, ALU.mult, ALU.subtract)

            for n, (_, parts, _, _) in enumerate(SMALL):
                dve.wait_ge(small_hi, n + 1)
                low(parts[1][:, :], RAW[n], S_W, parts[0][:, :]).then_inc(small_lo, 1)

            def patch_lo(t, u, slot, k):
                dve.wait_ge(xh_done, DONE(t))
                low(xhl(u, 1), xs(slot, k), S_X, xhl(u, 0)).then_inc(xl_done, 1)

            def stats(t, st):
                nc.vector.bn_stats(ST[:, ds(t * 6, 6)], htile(t)).then_inc(st, 1)

            def variances(st, mv):
                s = ST[:, :].rearrange("p (t c) -> p t c", c=6)
                dve.wait_ge(st, DONE(NT - 1))
                nc.vector.tensor_tensor(MEAN[:, :], s[:, :, 1], s[:, :, 4], ALU.add).then_inc(mv, 1)
                nc.vector.tensor_tensor(DM[:, :], s[:, :, 1], s[:, :, 4], ALU.subtract).then_inc(mv, 1)
                nc.vector.tensor_tensor(VAR[:, :], s[:, :, 2], s[:, :, 5], ALU.add).then_inc(mv, 1)
                dve.wait_ge(mv, 3)
                nc.vector.tensor_scalar(MEAN[:, :], MEAN[:, :], 0.5, None, ALU.mult).then_inc(mv, 1)
                nc.vector.scalar_tensor_tensor(DM[:, :], DM[:, :], 0.25 * C, DM[:, :], ALU.mult, ALU.mult).then_inc(mv, 1)
                dve.wait_ge(mv, 5)
                nc.vector.tensor_tensor(VAR[:, :], VAR[:, :], DM[:, :], ALU.add).then_inc(mv, 1)

            patch_lo(0, 0, 0, 0)
            patch_lo(1, 1, 0, 1)
            with dve.Fori(0, (NT - 2) // 4) as i:
                for v in range(4):
                    t, ahead = i * 4 + (1 + v), v + 2
                    dve.wait_ge(h_done, DONE(t - 1))
                    patch_lo(t + 1, ahead % 2, ahead // 2 % 2, ahead % 2)
                    stats(t - 1, st_done)
            dve.wait_ge(h_done, DONE(NT - 1))
            stats(NT - 2, st_done)
            stats(NT - 1, st_done)
            variances(st_done, mv_done)

            def norm_row(N, t, u):
                dve.wait_ge(N[2], FREE2(t))
                nc.vector.tensor_scalar(XF[:, u * C:(u + 1) * C], htile(t), MEAN[:, ds(t, 1)], RS[:, ds(t, 1)],
                                        ALU.subtract, ALU.mult).then_inc(N[0], 1)

            def norm_lo(N, t, u):
                dve.wait_ge(N[1], DONE(t))
                nc.vector.tensor_tensor(row_part(N, t, u, C, C), XF[:, u * C:(u + 1) * C],
                                        row_part(N, t, u, 0, C), ALU.subtract).then_inc(N[2], 1)

            def norm(N, sd, rs):
                dve.wait_ge(sd, 1)
                nc.vector.reciprocal(RS[:, :], RS[:, :]).then_inc(rs, 1)
                dve.wait_ge(rs, 1)
                norm_row(N, 0, 0)

            norm(N1, sd_done, rs_done)
            with dve.Fori(0, (NT - 2) // 2) as i:
                for u in range(2):
                    norm_row(N1, i * 2 + (u + 1), 1 - u)
                    norm_lo(N1, i * 2 + u, u)
            norm_row(N1, NT - 1, 1)
            norm_lo(N1, NT - 2, 0)
            norm_lo(N1, NT - 1, 1)

            def qkv_lo(t, u):
                dve.wait_ge(qh_done, DONE(t))
                dve.wait_ge(kh_done, DONE(t))
                qk = bank(0, HC, 4 * TT)
                low(diag(QM[1], u, 2), qk[:, 0:2 * TT].rearrange("p (b q) -> p b q", q=T), S_Q / S_XW, diag(QM[0], u, 2)).then_inc(ql_done, 1)
                kp = [KP[p][:, u * 2 * TT:(u + 1) * 2 * TT] for p in range(2)]
                low(kp[1], qk[:, 2 * TT:4 * TT], S_Q / S_XW, kp[0]).then_inc(kl_done, 1)
                dve.wait_ge(vh_done, DONE(t))
                low(VP[1][:, u * C:(u + 1) * C], bank(1, TT, C), S_V / S_XW, VP[0][:, u * C:(u + 1) * C]).then_inc(vl_done, 1)
                dve.wait_ge(s_mm, FREE2(t))
                nc.vector.tensor_tensor(
                    kbd(0, u).rearrange("p (c h k) -> p c h k", c=2, h=HH),
                    kp[0].rearrange("p (c k) -> p c k", c=2).unsqueeze(2).to_broadcast([HC, 2, HH, TT]),
                    HM[:, :].rearrange("p (h k) -> p h k", h=HH).unsqueeze(1).to_broadcast([HC, 2, HH, TT]),
                    ALU.mult).then_inc(kbh_done, 1)

            def shift(t, u):
                dve.wait_ge(s_mm, DONE(t))
                dve.wait_ge(sub_done, FREE2(t))
                mx = MX[:, u * HEADS:(u + 1) * HEADS]
                nc.vector.tensor_reduce(mx, heads(bank(2, TT, HEADS * T)), AX.X, ALU.max).then_inc(mx_done, 1)
                dve.wait_ge(mx_done, DONE(t))
                dve.wait_ge(pt_mm, FREE2(t))
                nc.vector.tensor_tensor(heads(PR[:, u * HEADS * T:(u + 1) * HEADS * T]), heads(bank(2, TT, HEADS * T)),
                                        mx.unsqueeze(2).to_broadcast([TT, HEADS, T]), ALU.subtract).then_inc(sub_done, 1)

            def values(t, u):
                dve.wait_ge(vr_mm, DONE(t))
                dve.wait_ge(o_mm, FREE2(t))
                for p, done in ((0, vbh_done), (1, vbl_done)):
                    nc.vector.tensor_tensor(
                        vbd(p, u).rearrange("p (b g c) -> p b g c", b=TI, g=NG)[:, :, :, 0:GC],
                        PSA[0:KEYS, 4 * 512:7 * 512].rearrange("p (b c) -> p b c", b=TI)[:, :, p * C:(p + 1) * C].rearrange("p b (g c) -> p b g c", g=NG),
                        VM[:, :].rearrange("p (g c) -> p g c", g=NG).unsqueeze(1).to_broadcast([KEYS, TI, NG, GC]),
                        ALU.mult).then_inc(done, 1)

            def probs_lo(t, u):
                dve.wait_ge(pth_done, DONE(t))
                low(diag(PT[1], u, NG), bank(3, KEYS, NG * TT).rearrange("p (b q) -> p b q", q=T), S_P, diag(PT[0], u, NG)).then_inc(ptl_done, 1)

            def outputs(t, u):
                dve.wait_ge(o_mm, DONE(t))
                o = bank(7, TT, NG * VC).rearrange("p (g c) -> p g c", g=NG)
                rd = RD[:, u * HEADS:(u + 1) * HEADS].rearrange("p (g h) -> p g h", g=NG)
                dve.wait_ge(yf_done, FREE2(t))
                nc.vector.reciprocal(rd, o[:, :, GC:VC]).then_inc(rd_done, 1)
                dve.wait_ge(rd_done, DONE(t))
                dve.wait_ge(yl_done, FREE2(t))
                nc.vector.tensor_tensor(
                    YF[:, u * C:(u + 1) * C].rearrange("p (g h d) -> p g h d", g=NG, h=GH),
                    o[:, :, 0:GC].rearrange("p g (h d) -> p g h d", h=GH),
                    rd.unsqueeze(3).to_broadcast([TT, NG, GH, HD]), ALU.mult).then_inc(yf_done, 1)

            dve.wait_ge(const_in, 16 * len(CONSTS))
            dve.wait_ge(consts_set, FILLS)
            qkv_lo(0, 0)
            shift(0, 0)
            values(0, 0)
            qkv_lo(1, 1)
            probs_lo(0, 0)
            with dve.Fori(0, (NT - 2) // 2) as i:
                for u in range(2):
                    t = i * 2 + (1 + u)
                    shift(t, 1 - u)
                    outputs(t - 1, u)
                    values(t, 1 - u)
                    qkv_lo(t + 1, u)
                    probs_lo(t, 1 - u)
            shift(NT - 1, 1)
            outputs(NT - 2, 0)
            values(NT - 1, 1)
            probs_lo(NT - 1, 1)
            outputs(NT - 1, 1)

            def residual(t, u):
                dve.wait_ge(op_mm, DONE(t))
                nc.vector.scalar_tensor_tensor(htile(t), bank(2 + u, TT, C), 1 / S_XW, htile(t), ALU.mult, ALU.add).then_inc(h2_done, 1)

            residual(0, 0)
            with dve.Fori(0, (NT - 2) // 2) as i:
                for u in range(2):
                    t = i * 2 + (1 + u)
                    dve.wait_ge(h2_done, DONE(t - 1))
                    residual(t, 1 - u)
                    stats(t - 1, st2_done)
            dve.wait_ge(h2_done, DONE(NT - 2))
            residual(NT - 1, 1)
            stats(NT - 2, st2_done)
            dve.wait_ge(h2_done, DONE(NT - 1))
            stats(NT - 1, st2_done)
            variances(st2_done, mv2_done)
            norm(N2, sd2_done, rs2_done)

            def logits(t, u):
                dve.wait_ge(r_mm, DONE(t))
                nc.vector.tensor_copy(LG[:, ds(t * E, E)], bank(4 + u, TT, E)).then_inc(lg_done, 1)

            norm_row(N2, 1, 1)
            norm_lo(N2, 0, 0)
            with dve.Fori(0, (NT - 2) // 2) as i:
                for u in range(2):
                    t = i * 2 + (1 + u)
                    norm_row(N2, t + 1, u)
                    norm_lo(N2, t, 1 - u)
                    logits(t - 1, u)
            norm_lo(N2, NT - 1, 1)
            logits(NT - 2, 0)
            logits(NT - 1, 1)

            dve.wait_ge(lg_done, DONE(NT - 1))
            dve.wait_ge(pt_mm, DONE(NT - 1))
            dve.wait_ge(w_lo, 2 * PIECES + 2)
            for t in range(NT):
                nc.vector.max(M8[:, t * E:(t + 1) * E], LG[:, t * E:(t + 1) * E]).then_inc(mx_done, 1)
            for t in range(NT):
                dve.wait_ge(mx_done, t + NT + 1 + CR)
                nc.vector.max_index(I8[:, t * E:(t + 1) * E], M8[:, t * E:(t + 1) * E], LG[:, t * E:(t + 1) * E]).then_inc(lg_done, 1)
            dve.wait_ge(lg_done, 2 * NT + CR)
            m8 = M8.rearrange("p (t e) -> p t e", e=E)
            i8 = I8.rearrange("p (t e) -> p t e", e=E)
            col = [RT[:, n * NT:(n + 1) * NT] for n in range(8)]
            nc.vector.tensor_tensor(col[0], m8[:, :, 1], m8[:, :, 0], ALU.subtract).then_inc(route, 1)
            for k in range(2):
                nc.vector.tensor_copy(col[2 + k], i8[:, :, k]).then_inc(route, 1)
            dve.wait_ge(route, 3)
            for k in range(2):
                nc.vector.tensor_tensor(OH[k].rearrange("p (t e) -> p t e", e=E), EID[:, :].unsqueeze(1).to_broadcast([TT, NT, E]),
                                        col[2 + k].unsqueeze(2).to_broadcast([TT, NT, E]), ALU.is_equal).then_inc(route, 1)
            def routed(n):
                dve.wait_ge(route, n)

            own3 = [OH[k].rearrange("p (t e) -> p t e", e=E) for k in range(2)]
            routed(5)
            dve.wait_ge(later_in, 16 * len(LATER))
            nc.vector.tensor_tensor(CHOSEN, OH[0], OH[1], ALU.add).then_inc(route, 1)
            routed(6)
            last = CHOSEN[:, (NT - 1) * E:NT * E]
            nc.vector.tensor_scalar(last, last, REAL[:, 0:1], None, ALU.mult).then_inc(route, 1)
            carry = RB.rearrange("p (t c) -> p t c", c=ROW)
            dve.wait_ge(gap_exp, 1)
            nc.vector.tensor_scalar(col[4], col[1], 1.0, S_G * S_W, ALU.add, ALU.mult).then_inc(route, 1)
            routed(8)
            nc.vector.reciprocal(col[4], col[4]).then_inc(route, 1)
            routed(9)
            nc.vector.tensor_tensor(col[5], col[4], col[1], ALU.mult).then_inc(route, 1)
            routed(10)
            nc.vector.tensor_tensor(carry[:, :, GAP], col[4], col[5], ALU.subtract).then_inc(route, 1)
            nc.vector.tensor_copy(carry[:, :, SECOND], col[5]).then_inc(route, 1)
            nc.vector.tensor_copy(carry[:, :, FIRST], col[2]).then_inc(route, 1)
            nc.vector.tensor_copy(carry[:, :, TOKEN], TOKENS).then_inc(route, 1)
            dve.wait_ge(rank_mm, 1)
            dve.wait_ge(ones_set, 3)
            nc.vector.tensor_scalar(CNTI, bank(7, ST_, E), float(ST_ - 1), None, ALU.add).then_inc(count, 1)
            dve.wait_ge(count, 1)
            nc.vector.tensor_scalar(CNTI, CNTI, 7, None, ALU.logical_shift_right).then_inc(count, 1)
            dve.wait_ge(count, 2)
            nc.vector.tensor_copy(CUM[0][:, E:2 * E], CNTI).then_inc(count, 1)
            for n, d in enumerate((1, 2, 4)):
                dve.wait_ge(count, 3 + n)
                a = CUM[n % 2]
                nc.vector.tensor_tensor(CUM[1 - n % 2][:, E:2 * E], a[:, E:2 * E], a[:, E - d:2 * E - d], ALU.add).then_inc(count, 1)
            dve.wait_ge(count, 6)
            cum = CUM[1]
            nc.vector.tensor_scalar(START, cum[:, E - 1:2 * E - 1], float(ST_), None, ALU.mult).then_inc(count, 1)
            passed = PASSED.rearrange("p (s e) -> p s e", e=E - 1)
            nc.vector.tensor_tensor(passed, TILENO.unsqueeze(2).to_broadcast([ST_, NS, E - 1]),
                                    cum[:, E:2 * E - 1].unsqueeze(1).to_broadcast([ST_, NS, E - 1]), ALU.is_ge).then_inc(count, 1)
            dve.wait_ge(count, 7)
            nc.vector.tensor_tensor(SLOTS.rearrange("p (t e) -> p t e", e=E), bank(6, TT, NT * E).rearrange("p (t e) -> p t e", e=E),
                                    START[0:TT].unsqueeze(1).to_broadcast([TT, NT, E]), ALU.add).then_inc(count, 1)
            dve.wait_ge(count, 9)
            nc.vector.tensor_reduce(EXPF, passed, AX.X, ALU.add).then_inc(count, 1)
            for k in range(2):
                nc.vector.tensor_tensor(OWN[k], OH[k], SLOTS, ALU.mult).then_inc(count, 1)
            for k in range(2):
                dve.wait_ge(count, 11 + k)
                nc.vector.tensor_reduce(col[6 + k], OWN[k].rearrange("p (t e) -> p t e", e=E), AX.X, ALU.add).then_inc(count, 1)
            dve.wait_ge(count, 14)
            nc.vector.tensor_copy(SLOTI, RT[:, 6 * NT:8 * NT]).then_inc(route, 1)
            nc.vector.tensor_copy(EXPI, EXPF).then_inc(count, 1)

            def rows_out(s, u):
                dve.wait_ge(xr_mm, DONE(s))
                dve.wait_ge(up_mm, FREE2(s))
                nc.vector.tensor_copy(YT[0:HC, u * 4 * ST_:(u + 1) * 4 * ST_], bank(6 + u, HC, 4 * ST_, F16)).then_inc(xt_done, 1)

            def hidden_lo(s, u):
                dve.wait_ge(gh_done, DONE(s))
                g = slice(u * F, (u + 1) * F)
                low(GP[1][:, g], G[:, g], S_G, GP[0][:, g]).then_inc(gl_done, 1)

            def gates(s, u, landed, waits=True):
                dve.wait_ge(meta_in[u], landed)
                if waits:
                    dve.wait_ge(y_added, ADDED(s - 1))
                dve.wait_ge(y_done, FREE2(s))
                nc.vector.tensor_tensor(MATCH[u], XM[u][:, 1:2], EXPF[:, ds(s, 1)], ALU.is_equal).then_inc(match_done, 1)
                nc.vector.tensor_copy(IDX[u], XM[u][:, 0:1]).then_inc(match_done, 1)
                dve.wait_ge(match_done, 2 * s + 2)
                nc.vector.scalar_tensor_tensor(GATE[u], MATCH[u], XM[u][:, 2:3], XM[u][:, 3:4], ALU.mult, ALU.add).then_inc(gate_done, 1)

            def gated(s, u):
                dve.wait_ge(down_mm, DONE(s))
                dve.wait_ge(gate_done, DONE(s))
                nc.vector.tensor_scalar(YO[u], bank(4 + u, ST_, C), GATE[u][:, 0:1], None, ALU.mult).then_inc(y_done, 1)

            dve.wait_ge(count, 15)
            rows_out(0, 0)
            gates(0, 0, 16, False)
            rows_out(1, 1)
            hidden_lo(0, 0)

            def step(s, u, landed, waits=True):
                rows_out(s + 2, u)
                hidden_lo(s + 1, 1 - u)
                gated(s, u)
                gates(s + 1, 1 - u, landed, waits)

            step(0, 0, 16, False)
            with dve.Fori(0, (NS - 3) // 2) as i:
                for v in (1, 2):
                    step(i * 2 + v, v % 2, i * 16 + 32)
            hidden_lo(NS - 1, 0)
            gated(NS - 2, 1)
            gates(NS - 1, 0, 16 * (NS // 2 + 1))
            gated(NS - 1, 0)

        @block.tensor
        def _(pe):
            for s in (emb_mm, N1[3], qk_mm, v_mm, s_mm, pt_mm, vr_mm, o_mm, yt_mm, op_mm, N2[3], r_mm, up_mm, down_mm, xr_mm):
                pe.sem_inc(s, CR)

            def embed(t, u):
                pe.wait_ge(xl_done, DONE(t))
                pe.wait_ge(h_done, FREE2(t))
                n = 0
                for k in range(KT):
                    for a, b in PRODUCTS:
                        ins = nc.tensor.matmul(bank(u, TT, C), xhl(u, a)[:, k * TT:(k + 1) * TT], WT[b][:, k * C:(k + 1) * C],
                                               start=n == 0, stop=n == 3 * KT - 1)
                        n += 1
                ins.then_inc(emb_mm, 1)

            pe.wait_ge(small_lo, 1)
            with pe.Fori(0, NT // 2) as i:
                for u in range(2):
                    embed(i * 2 + u, u)

            def norm_transpose(N, t, u):
                pe.wait_ge(N[2], DONE(t))
                pe.wait_ge(N[4], FREE2(t))
                for p in range(2):
                    for c in range(2):
                        n = 2 * p + c
                        ins = nc.tensor.transpose(bank(2 + u, HC, 4 * TT, F16)[:, n * TT:(n + 1) * TT],
                                                  row_part(N, t, u, n * HC, HC), IDH[0:TT, 0:TT])
                ins.then_inc(N[3], 1)

            pe.wait_ge(const_in, 16 * len(CONSTS))
            with pe.Fori(0, NT // 2) as i:
                for u in range(2):
                    norm_transpose(N1, i * 2 + u, u)

            def qkv(t, u):
                pe.wait_ge(N1[4], DONE(t))
                pe.wait_ge(ql_done, FREE1(t))
                pe.wait_ge(kl_done, FREE1(t))
                for j in range(4):
                    n = 0
                    for c in range(2):
                        for a, b in PRODUCTS:
                            ins = nc.tensor.matmul(bank(0, HC, 4 * TT)[:, j * TT:(j + 1) * TT],
                                                   WA[a][:, c * 3 * C + j * HC:c * 3 * C + (j + 1) * HC], xn(t, b, c), start=n == 0, stop=n == 5)
                            n += 1
                ins.then_inc(qk_mm, 1)
                pe.wait_ge(vl_done, FREE1(t))
                n = 0
                for c in range(2):
                    for a, b in PRODUCTS:
                        ins = nc.tensor.matmul(bank(1, TT, C), xn(t, a, c), WA[b][:, c * 3 * C + 2 * C:(c + 1) * 3 * C], start=n == 0, stop=n == 5)
                        n += 1
                ins.then_inc(v_mm, 1)

            def scores(t, u):
                pe.wait_ge(ql_done, DONE(t))
                pe.wait_ge(kbh_done, DONE(t))
                pe.wait_ge(kbl_done, DONE(t))
                pe.wait_ge(sub_done, FREE1(t))
                nc.tensor.matmul(bank(2, TT, HEADS * T), SELQ[:, :], CAUS[:, :].unsqueeze(1).to_broadcast([T, HEADS, T]), start=True, stop=False)
                for c in range(2):
                    for b in range(TI):
                        for p, q in PRODUCTS:
                            at = (2 * u + c) * DW + b * TT
                            keys = kbd(q, u).rearrange("p (c h k) -> p c h k", c=2, h=HH)[:, c, :, b * T:(b + 1) * T]
                            ins = nc.tensor.matmul(bank(2, TT, HEADS * T)[:, c * HH * T:(c + 1) * HH * T], QM[p][:, at:at + TT], keys,
                                                   start=False, stop=(c, b, p) == (1, TI - 1, 1))
                ins.then_inc(s_mm, 1)

            def transpose_probs(t, u):
                pe.wait_ge(p_done, DONE(t))
                pe.wait_ge(ptl_done, FREE1(t))
                for g in range(NG):
                    at = u * HEADS * T + g * KEYS
                    ins = nc.tensor.transpose(bank(3, KEYS, NG * TT)[:, g * TT:(g + 1) * TT], PR[:, at:at + KEYS], IDF[0:TT, 0:TT])
                ins.then_inc(pt_mm, 1)

            def spread_values(t, u):
                pe.wait_ge(vl_done, DONE(t))
                pe.wait_ge(vbl_done, FREE1(t))
                for b in range(TI):
                    for p in range(2):
                        ins = nc.tensor.matmul(bank(4 + b, KEYS, 2 * C)[:, p * C:(p + 1) * C], SELV[:, b * KEYS:(b + 1) * KEYS],
                                               VP[p][:, u * C:(u + 1) * C], start=True, stop=True)
                ins.then_inc(vr_mm, 1)

            def outputs(t, u):
                pe.wait_ge(ptl_done, DONE(t))
                pe.wait_ge(vbl_done, DONE(t))
                pe.wait_ge(yf_done, FREE1(t))
                for g in range(NG):
                    n = 0
                    for b in range(TI):
                        for p, q in PRODUCTS:
                            at = (u * NG + g) * DW + b * TT
                            vat = (b * NG + g) * VC
                            ins = nc.tensor.matmul(bank(7, TT, NG * VC)[:, g * VC:(g + 1) * VC], PT[p][:, at:at + TT],
                                                   vbd(q, u)[:, vat:vat + VC], start=n == 0, stop=n == 3 * TI - 1)
                            n += 1
                ins.then_inc(o_mm, 1)

            pe.wait_ge(small_lo, len(SMALL))
            pe.wait_ge(consts_set, FILLS)
            pe.wait_ge(h_done, DONE(NT - 1))
            pe.wait_ge(N1[4], DONE(NT - 1))
            qkv(0, 0)
            scores(0, 0)
            spread_values(0, 0)
            qkv(1, 1)
            transpose_probs(0, 0)
            with pe.Fori(0, (NT - 2) // 2) as i:
                for u in range(2):
                    t = i * 2 + (1 + u)
                    scores(t, 1 - u)
                    outputs(t - 1, u)
                    spread_values(t, 1 - u)
                    qkv(t + 1, u)
                    transpose_probs(t, 1 - u)
            scores(NT - 1, 1)
            outputs(NT - 2, 0)
            spread_values(NT - 1, 1)
            transpose_probs(NT - 1, 1)
            outputs(NT - 1, 1)

            def transpose_y(t, u):
                pe.wait_ge(yl_done, DONE(t))
                pe.wait_ge(yt_done, FREE2(t))
                for p in range(2):
                    for c in range(2):
                        n = 2 * p + c
                        ins = nc.tensor.transpose(bank(u, HC, 4 * TT, F16)[:, n * TT:(n + 1) * TT], Y[p][:, ds(t * C + c * HC, HC)], IDH[0:TT, 0:TT])
                ins.then_inc(yt_mm, 1)

            def project(t, u):
                pe.wait_ge(yt_done, DONE(t))
                pe.wait_ge(h2_done, FREE2(t))
                n = 0
                for c in range(2):
                    for a, b in PRODUCTS:
                        at = u * 4 * ST_ + (2 * a + c) * ST_
                        ins = nc.tensor.matmul(bank(2 + u, TT, C), YT[:, at:at + TT], WO[b][:, c * C:(c + 1) * C], start=n == 0, stop=n == 5)
                        n += 1
                ins.then_inc(op_mm, 1)

            pe.wait_ge(ptl_done, DONE(NT - 1))
            pe.wait_ge(vl_done, DONE(NT - 1))
            transpose_y(0, 0)
            with pe.Fori(0, (NT - 2) // 2) as i:
                for u in range(2):
                    transpose_y(i * 2 + (u + 1), 1 - u)
                    project(i * 2 + u, u)
            transpose_y(NT - 1, 1)
            project(NT - 2, 0)
            project(NT - 1, 1)

            def router(t, u):
                pe.wait_ge(N2[4], DONE(t))
                pe.wait_ge(lg_done, FREE2(t))
                n = 0
                for c in range(2):
                    for a, b in PRODUCTS:
                        ins = nc.tensor.matmul(bank(4 + u, TT, E), xn(t, a, c)[0:HC], WR[b][:, c * E:(c + 1) * E], start=n == 0, stop=n == 5)
                        n += 1
                ins.then_inc(r_mm, 1)

            pe.wait_ge(h2_done, DONE(NT - 1))
            norm_transpose(N2, 0, 0)
            with pe.Fori(0, (NT - 2) // 2) as i:
                for u in range(2):
                    norm_transpose(N2, i * 2 + (u + 1), 1 - u)
                    router(i * 2 + u, u)
            norm_transpose(N2, NT - 1, 1)
            router(NT - 2, 0)
            router(NT - 1, 1)

            pe.wait_ge(route, 7)
            pe.wait_ge(ones_set, 1)
            pe.wait_ge(later_in, 16 * len(LATER))
            nc.tensor.matmul(bank(6, TT, NT * E), BEFORE[:, 0:TT], CHOSEN, start=True, stop=False)
            for d in range(1, NT):
                nc.tensor.matmul(bank(6, TT, NT * E)[:, d * E:NT * E], ONES[:, 0:TT], CHOSEN[:, 0:(NT - d) * E], start=False, stop=d == NT - 1)
            for t in range(NT):
                ins = nc.tensor.matmul(bank(7, ST_, E), ONES, CHOSEN[:, t * E:(t + 1) * E], start=t == 0, stop=t == NT - 1)
            ins.then_inc(rank_mm, 1)

            def transpose_rows(s, u, landed):
                pe.wait_ge(rows_in[u], landed)
                pe.wait_ge(xt_done, FREE2(s))
                x = XR[u].bitcast(F16)
                for n in range(4):
                    ins = nc.tensor.transpose(bank(6 + u, HC, 4 * ST_, F16)[:, n * ST_:(n + 1) * ST_], x[:, n * HC:(n + 1) * HC], IDH[:, :])
                ins.then_inc(xr_mm, 1)

            def up(s, u, e):
                pe.wait_ge(xt_done, DONE(s))
                pe.wait_ge(gelu_done, FREE2(s))
                for f in range(FC):
                    w = f % (FC // 2) * ST_
                    k = 0
                    for c in range(2):
                        for a, b in PRODUCTS:
                            at = u * 4 * ST_ + (2 * b + c) * ST_
                            ins = nc.tensor.matmul(bank(2 * u + f // (FC // 2), 128, FC // 2 * ST_)[:, w:w + ST_],
                                                   W1[a][:, ds(e * (2 * F) + (c * F + f * 128), 128)], YT[:, at:at + ST_], start=k == 0, stop=k == 5)
                            k += 1
                ins.then_inc(up_mm, 1)

            def down(s, u, e):
                pe.wait_ge(gl_done, DONE(s))
                pe.wait_ge(y_done, FREE2(s))
                for f in range(FC):
                    for a, b in PRODUCTS:
                        at = (u * FC + f) * ST_
                        nc.tensor.matmul(bank(4 + u, ST_, C), GP[a][:, at:at + ST_], W2[b][:, ds(e * W2E + f * C, C)],
                                         start=(f, a, b) == (0, 0, 0), stop=False)
                for p in range(2):
                    ins = nc.tensor.matmul(bank(4 + u, ST_, C), ONE[:, :], W2[p][0:1, ds(e * W2E + FC * C, C)], start=False, stop=p == 1)
                ins.then_inc(down_mm, 1)

            def experts(s, n):
                return nc.values_load_multi_w_load_instructions(EXPI[0:1, ds(s, n)], [mybir.EngineType.PE],
                                                                min_val=0, max_val=E - 1)[1]

            pe.wait_ge(count, 15)
            pe.wait_ge(route, ROUTED)
            transpose_rows(0, 0, 16)
            transpose_rows(1, 1, 16)
            up(0, 0, experts(0, 1)[0])
            with pe.Fori(0, (NS - 3) // 4) as i:
                e = experts(i * 4, 5)
                for v in range(4):
                    s, u = i * 4 + v, v % 2
                    up(s + 1, 1 - u, e[v + 1])
                    transpose_rows(s + 2, u, i * 32 + (32 if v < 2 else 48))
                    down(s, u, e[v])
            e = experts(NS - 3, 3)
            up(NS - 2, 1, e[1])
            transpose_rows(NS - 1, 0, 16 * (NS // 2 + 1))
            down(NS - 3, 0, e[0])
            up(NS - 1, 0, e[2])
            down(NS - 2, 1, e[1])
            down(NS - 1, 0, e[2])


def kernel(**inputs):
    import ml_dtypes
    import concourse.bacc as bacc
    from concourse.bass_utils import run_bass_kernel_spmd

    def arr(name):
        return np.asarray(inputs[name])

    def ones_row(w, bias):
        cols = w.shape[1]
        r = np.zeros((HC + 1, 2, cols), w.dtype)
        r[0:HC] = w.reshape(2, HC, cols).transpose(1, 0, 2)
        r[HC, 1] = bias
        return r.reshape(HC + 1, 2 * cols)

    x = arr("x").reshape(B, CIN, SIDE, PATCH, SIDE, PATCH).transpose(0, 2, 4, 3, 5, 1).reshape(B * T, DTOK)
    xp = np.zeros((NT * TT, DTOK), x.dtype)
    xp[0:B * T] = x
    w1 = arr("L0_ffn_w1")
    w1p = np.stack([ones_row(w1[e], arr("L0_ffn_b1")[e]) for e in range(E)], 1)
    w2 = arr("L0_ffn_w2")
    w2p = np.zeros((128, E, FC + 1, C), w2.dtype)
    w2p[:, :, 0:FC] = w2.reshape(E, FC, 128, C).transpose(2, 0, 1, 3)
    w2p[0, :, FC] = arr("L0_ffn_b2")
    key = np.arange(KEYS)
    ch = np.arange(C)
    tok = np.arange(TT)
    data = {
        "xt": xp.reshape(NT, TT, KT, 128).transpose(0, 3, 2, 1).reshape(NT, 128, KT * TT),
        "wtok": arr("L0_tok_W").reshape(KT, 128, C).transpose(1, 0, 2).reshape(128, KT * C),
        "wqkv": ones_row(arr("L0_attn_W_attn").T, arr("L0_attn_b_attn")),
        "wo": ones_row(arr("L0_attn_W_o").T, arr("L0_attn_b_o")),
        "wr": arr("L0_ffn_router_w").T.reshape(2, HC, E).transpose(1, 0, 2).reshape(HC, 2 * E),
        "w1": w1p.reshape(HC + 1, E * 2 * F),
        "w2": w2p.reshape(128, E * (FC + 1) * C),
        "idf": np.eye(128, dtype=np.float32),
        "idh": np.eye(128, dtype=np.float16),
        "selq": (np.arange(T)[:, None] == tok[None, :] % T).astype(ml_dtypes.bfloat16),
        "causal": np.where(np.arange(T)[:, None] >= np.arange(T)[None, :], 0.0, -1e30).astype(ml_dtypes.bfloat16),
        "selv": np.stack([tok[:, None] == b * T + key[None, :] % T for b in range(TI)], 1).reshape(TT, TI * KEYS).astype(np.float16),
        "hmask": np.repeat(np.arange(HC)[:, None] // HD == np.arange(HH)[None, :], TT, 1).astype(np.float16),
        "vmask": (key[:, None] // T == ch[None, :] // HD % GH).astype(np.float32),
        "vones": (key[:, None] // T == np.arange(GH)[None, :]).astype(np.float16),
        "before": (tok[:, None] < np.arange(128)[None, :]).astype(np.float16),
        "tileno": np.tile(np.arange(NS), (ST_, 1)).astype(np.float32),
        "tokens": (np.arange(NT)[None, :] * TT + tok[:, None]).astype(np.float32),
        "real": (tok[:, None] < LAST).astype(np.float32),
        "empty": np.concatenate([np.zeros((ST_, C)), B * T + np.arange(ST_)[:, None], -np.ones((ST_, 1)), np.zeros((ST_, 2))], 1).astype(np.float32),
        "eid": np.tile(np.arange(E), (TT, 1)).astype(np.float32),
    }
    nc = bacc.Bacc("TRN2", target_bir_lowering=False, num_devices=1)
    arrays, args = {}, []
    for name in ("eid", "before", "tileno", "tokens", "real", "empty"):
        data[name] = data.pop(name)
    for name, a in data.items():
        arrays[name] = np.ascontiguousarray(a)
        args.append(nc.dram_tensor(name, a.shape, mybir.dt.from_np(a.dtype), kind="ExternalInput").ap())
    args.append(nc.dram_tensor("slots", (NS * ST_, ROW), F32, kind="Internal").ap())
    args.append(nc.dram_tensor("out", (B * T + DUMP, C), F32, kind="ExternalOutput").ap())
    build(nc, *args)
    r = run_bass_kernel_spmd(nc, [arrays], core_ids=[0])
    return np.asarray(r.results[0]["out"])[0:B * T].reshape(B, T, C)
```

```python
from contextlib import ExitStack

import numpy as np
import concourse.bass as bass
from concourse import mybir

F32 = mybir.dt.float32
F16 = mybir.dt.float16
BF16 = mybir.dt.bfloat16
U32 = mybir.dt.uint32
ALU = mybir.AluOpType
ACT = mybir.ActivationFunctionType
AX = mybir.AxisListType

B, CIN, IMG, PATCH = 64, 3, 96, 16
SIDE = IMG // PATCH
T = SIDE * SIDE
C, HEADS = 192, 12
HD = C // HEADS
E, F = 8, 768
DTOK = CIN * PATCH * PATCH
KT = DTOK // 128

TI = 3
TT = TI * T
NT = -(-B // TI)
HC = C // 2
HH = HEADS // 2
GH = 3
NG = HEADS // GH
KEYS = GH * T
GC = GH * HD
VC = GC + GH
FC = F // 128
LAST = B * T - (NT - 1) * TT

TOPK = 2
ST_ = 128
NS = TOPK * B * T // ST_ + E - 1
ROW = C + 4
TOKEN, FIRST, GAP, SECOND = range(C, ROW)
DUMP = ST_

S_X, S_W = 2.0 ** 8, 2.0 ** 10
S_XW = S_X * S_W
S_Q, S_V, S_P, S_G = 2.0 ** 6, 2.0 ** 8, 2.0 ** 12, 2.0 ** 6
EPS = 1e-5
PRODUCTS = [(0, 0), (0, 1), (1, 0)]

CR = 2


def DONE(t):
    return t + 1 + CR


def FREE2(t):
    return t + 1


def ADDED(n):
    return 16 * n


def FREE1(t):
    return t + CR


def build(nc, xt, wtok, wqkv, wo, wr, w1, w2, idf, idh, selq, causal, selv, hmask, vmask, vones, eid,
          before, tileno, tokens, real, empty, slots, out):
    ds = bass.ds
    ctx = ExitStack()
    with ctx:
        def sb(name, shape, dt=F32):
            return ctx.enter_context(nc.sbuf_tensor(name, shape, dt))

        def sem(name):
            return ctx.enter_context(nc.semaphore(name))

        H = sb("H", [TT, NT * C])
        XN = sb("XN", [HC + 1, NT * 4 * TT], F16)
        W1 = [sb(f"W1{p}", [HC + 1, E * 2 * F], F16) for p in "hl"]
        W2E = FC * C + C
        W2 = [sb(f"W2{p}", [128, E * W2E], F16) for p in "hl"]
        ST = sb("ST", [TT, NT * 6])
        MEAN = sb("MEAN", [TT, NT])
        VAR = sb("VAR", [TT, NT])
        DM = sb("DM", [TT, NT])
        SCALE = sb("SCALE", [128, 1])
        RS = sb("RS", [TT, NT])
        EPSV = sb("EPSV", [TT, 1])
        ONE = sb("ONE", [1, 128], F16)
        IDF = sb("IDF", [128, 128])
        IDH = sb("IDH", [128, 128], F16)
        SELQ = sb("SELQ", [T, TT], BF16)
        CAUS = sb("CAUS", [T, T], BF16)
        SELV = sb("SELV", [TT, TI * KEYS], F16)
        HM = sb("HM", [HC, HH * TT], F16)
        VM = sb("VM", [KEYS, C])
        VO = sb("VO", [KEYS, GH], F16)
        EID = sb("EID", [TT, E])
        WA = [sb(f"WA{p}", [HC + 1, 2 * 3 * C], F16) for p in "hl"]
        WO = [sb(f"WO{p}", [HC + 1, 2 * C], F16) for p in "hl"]
        WR = [sb(f"WR{p}", [HC, 2 * E], F16) for p in "hl"]
        WSTG = sb("WSTG", [128, 2 * F])
        REG = sb("REG", [128, max(6 * KT * TT, NT * ROW)])
        XW = KT * TT
        XHL = REG[:, 4 * XW:6 * XW].bitcast(F16)
        Y = [REG[0:TT, p * NT * C // 2:(p + 1) * NT * C // 2].bitcast(F16) for p in range(2)]
        RB = REG[0:TT, 0:NT * ROW]
        RBH = RB.bitcast(F16)
        KW = 2 * HH * TT
        KBR = sb("KBR", [128, 2 * KW])
        KB = [KBR[0:HC, p * KW:(p + 1) * KW].bitcast(F16) for p in range(2)]
        WT = [KBR[:, p * KT * C // 2:(p + 1) * KT * C // 2].bitcast(F16) for p in range(2)]
        cut = [0]

        def after(cols):
            cut[0] += cols
            return KBR[:, cut[0] - cols:cut[0]]

        XR = [after(C) for _ in range(2)]
        XM = [after(ROW - C) for _ in range(2)]
        YO = [after(C) for _ in range(2)]
        IDX = [after(1).bitcast(U32) for _ in range(2)]
        MATCH = [after(1) for _ in range(2)]
        GATE = [after(1) for _ in range(2)]
        BEFORE = after(64).bitcast(F16)[0:TT]
        ONES = after(64).bitcast(F16)[0:TT]
        TILENO, TOKENS, REAL = after(NS), after(NT)[0:TT], after(1)[0:TT]
        EXPF, EXPI = after(NS), after(NS).bitcast(mybir.dt.int32)
        PASSED = after(NS * (E - 1))
        CNTI = after(E).bitcast(mybir.dt.int32)
        CUM = [after(2 * E) for _ in range(2)]
        START = after(E)
        JUNK, JUNK2 = after(1), after(1)[0:1]
        DW = TI * (TT + T)
        PTR = sb("PTR", [128, 2 * NG * DW])
        PT = [PTR[0:KEYS, p * NG * DW:(p + 1) * NG * DW].bitcast(F16) for p in range(2)]
        SMALL = [(wtok, WT, 128, KT * C), (wqkv, WA, HC + 1, 6 * C), (wo, WO, HC + 1, 2 * C), (wr, WR, HC, 2 * E)]
        RAW, at = [], 0
        for _, _, rows, cols in SMALL:
            RAW.append(PTR[0:rows, at:at + cols])
            at += cols
        G = PTR[:, 0:2 * F]
        GP = [PTR[:, (2 + p) * F:(3 + p) * F].bitcast(F16) for p in range(2)]
        XF = sb("XF", [TT, 2 * C])
        XP = sb("XP", [TT, 2 * 2 * C], F16)
        QM = [sb(f"QM{p}", [HC, 2 * 2 * DW], F16) for p in "hl"]
        KP = [sb(f"KP{p}", [HC, 2 * 2 * TT], F16) for p in "hl"]
        VP = [sb(f"VP{p}", [TT, 2 * C], F16) for p in "hl"]
        VB = [sb(f"VB{p}", [KEYS, 2 * TI * NG * VC], F16) for p in "hl"]
        LG = VB[0][:, 0:2 * NT * E].bitcast(F32)
        MX = sb("MX", [TT, 2 * HEADS])
        PR = sb("PR", [TT, 2 * HEADS * T])
        RD = sb("RD", [TT, 2 * HEADS])
        YF = sb("YF", [TT, 2 * C])
        YT = sb("YT", [HC + 1, 2 * 4 * ST_], F16)
        M8 = PR[:, 0:NT * E]
        I8 = PR[:, NT * E:2 * NT * E].bitcast(U32)
        OH = [WSTG[0:TT, n * NT * E:(n + 1) * NT * E] for n in range(2)]
        OWN = [WSTG[0:TT, (2 + n) * NT * E:(3 + n) * NT * E] for n in range(2)]
        SLOTS = WSTG[0:TT, 4 * NT * E:5 * NT * E]
        CHOSEN = WSTG[0:TT, 5 * NT * E:5 * NT * E + NT * E // 2].bitcast(F16)
        RT = PR[:, 2 * NT * E:2 * NT * E + 8 * NT]
        SLOTI = PR[:, 2 * NT * E + 8 * NT:2 * NT * E + 10 * NT].bitcast(U32)

        PSA = ctx.enter_context(nc.psum_tensor("PSA", [128, 8 * 512], F32))

        def bank(n, rows, cols, dt=F32):
            v = PSA[0:rows, n * 512:(n + 1) * 512]
            return (v.bitcast(dt) if dt != F32 else v)[:, 0:cols]

        const_in, consts_set = sem("const_in"), sem("consts_set")
        raw_in = [sem(f"raw_in{n}") for n in range(4)]
        small_hi, small_lo = sem("small_hi"), sem("small_lo")
        pt_zero = sem("pt_zero")
        x_in = [sem(f"x_in{n}") for n in range(2)]
        xh_done, xl_done, emb_mm, h_done = [sem(n) for n in ("xh_done", "xl_done", "emb_mm", "h_done")]
        st_done, mv_done, sd_done, rs_done = [sem(n) for n in ("st_done", "mv_done", "sd_done", "rs_done")]
        N1 = [sem(f"norm1_{n}") for n in ("row", "hi", "lo", "transposed", "done")]
        qk_mm, v_mm = sem("qk_mm"), sem("v_mm")
        qh_done, kh_done, vh_done = sem("qh_done"), sem("kh_done"), sem("vh_done")
        ql_done, kl_done, vl_done = sem("ql_done"), sem("kl_done"), sem("vl_done")
        kbh_done, kbl_done = sem("kbh_done"), sem("kbl_done")
        s_mm, mx_done, sub_done, p_done = sem("s_mm"), sem("mx_done"), sem("sub_done"), sem("p_done")
        pt_mm, pth_done, ptl_done = sem("pt_mm"), sem("pth_done"), sem("ptl_done")
        vr_mm, vbh_done, vbl_done = sem("vr_mm"), sem("vbh_done"), sem("vbl_done")
        o_mm, rd_done, yf_done, yh_done, yl_done = [sem(n) for n in ("o_mm", "rd_done", "yf_done", "yh_done", "yl_done")]
        yt_mm, yt_done, op_mm, h2_done, st2_done, mv2_done = [sem(n) for n in ("yt_mm", "yt_done", "op_mm", "h2_done", "st2_done", "mv2_done")]
        sd2_done, rs2_done = sem("sd2_done"), sem("rs2_done")
        N2 = [sem(f"norm2_{n}") for n in ("row", "hi", "lo", "transposed", "done")]
        r_mm, lg_done = sem("r_mm"), sem("lg_done")
        route, gap_exp = sem("route"), sem("gap_exp")
        b2_in = sem("b2_in")
        w_in = [sem(f"w_in{n}") for n in range(2)]
        w_scaled, w_hi, w_lo = sem("w_scaled"), sem("w_hi"), sem("w_lo")
        later_in, ones_set, empty_in, h_stored = sem("later_in"), sem("ones_set"), sem("empty_in"), sem("h_stored")
        rank_mm, count, dispatched = sem("rank_mm"), sem("count"), sem("dispatched")
        rows_in = [sem(f"rows_in{n}") for n in range(2)]
        meta_in = [sem(f"meta_in{n}") for n in range(2)]
        match_done, gate_done, xr_mm, xt_done = sem("match_done"), sem("gate_done"), sem("xr_mm"), sem("xt_done")
        up_mm, gelu_done, gh_done, gl_done, down_mm, y_done = [sem(n) for n in ("up_mm", "gelu_done", "gh_done", "gl_done", "down_mm", "y_done")]
        y_added, add_turn = sem("y_added"), sem("add_turn")
        CONSTS = [(IDF, idf), (IDH, idh), (SELQ, selq), (CAUS, causal), (SELV, selv), (HM, hmask), (VM, vmask), (VO, vones), (EID, eid)]
        LATER = [(BEFORE, before), (TILENO, tileno), (TOKENS, tokens), (REAL, real)]
        ROUTED = 15
        FILLS = 12
        block = ctx.enter_context(nc.Block())

        def xs(slot, k):
            return REG[:, (2 * slot + k) * XW:(2 * slot + k + 1) * XW]

        def xhl(u, p):
            return XHL[:, (2 * u + p) * XW:(2 * u + p + 1) * XW]

        def htile(t):
            return H[:, ds(t * C, C)]

        def xn(t, p, c):
            return XN[:, ds(t * (4 * TT) + (2 * p + c) * TT, TT)]

        def diag(buf, u, n):
            return buf[:, u * n * DW:(u + 1) * n * DW].rearrange("p (b q) -> p b q", q=TT + T)[:, :, 0:T]

        def kbd(p, u):
            return KB[p][:, u * KW:(u + 1) * KW]

        def vbd(p, u):
            return VB[p][:, u * TI * NG * VC:(u + 1) * TI * NG * VC]

        def heads(ap):
            return ap.rearrange("p (h k) -> p h k", h=HEADS)

        def row_part(N, t, u, at, cols):
            return XP[:, u * 2 * C + at:u * 2 * C + at + cols] if N is N1 else RBH[:, ds(t * (2 * ROW) + at, cols)]

        PIECES = 2 * E
        N1_STEPS = (NT - 2) // 4
        W1_STEPS = PIECES // 2 - N1_STEPS
        W2_STEPS = (NT - 4) // 2 - W1_STEPS
        OP_STEPS = PIECES // 2 - W2_STEPS

        def w1_piece(work, i, u):
            at = (i * 2 + u) * F
            work(i * 2 + u, u, W1, at, WSTG[0:HC + 1, u * F:(u + 1) * F])

        def w2_piece(work, i, u):
            at = (i * 2 + u) * (W2E // 2)
            work(i * 2 + (u + PIECES), u, W2, at, WSTG[:, u * F:u * F + W2E // 2])

        @block.sync
        def _(sp):
            def patches(pair, slot):
                sp.dma_start(REG[:, slot * 2 * XW:(slot + 1) * 2 * XW].rearrange("p (t c) -> p t c", t=2),
                             xt[ds(pair * 2, 2), :, :].rearrange("t p c -> p t c")).then_inc(x_in[slot], 16)

            sp.dma_start(RAW[0], wtok).then_inc(raw_in[0], 16)
            patches(0, 0)
            patches(1, 1)
            for n in range(1, len(SMALL)):
                sp.dma_start(RAW[n], SMALL[n][0]).then_inc(raw_in[n], 16)
            for dst, src in CONSTS:
                sp.dma_start(dst[:, :], src).then_inc(const_in, 16)
            LOOPED = (NT // 2 - 3) // 2
            with sp.Fori(0, LOOPED) as i:
                for slot in range(2):
                    sp.wait_ge(xl_done, i * 4 + (2 * slot + 2 + CR))
                    patches(i * 2 + (2 + slot), slot)
            for pair in range(2 + 2 * LOOPED, NT // 2):
                sp.wait_ge(xl_done, 2 * (pair - 1) + CR)
                patches(pair, pair % 2)
            with sp.Fori(0, PIECES // 2) as i:
                for u in range(2):
                    sp.wait_ge(w_lo, i * 2 + (u + 1))
                    sp.dma_start(WSTG[0:HC + 1, u * F:(u + 1) * F], w1[:, ds((i * 2 + u) * F, F)]).then_inc(w_in[u], 16)
            with sp.Fori(0, PIECES // 2) as i:
                for u in range(2):
                    sp.wait_ge(w_lo, i * 2 + (PIECES + u + 1))
                    sp.dma_start(WSTG[:, u * F:u * F + W2E // 2], w2[:, ds((i * 2 + u) * (W2E // 2), W2E // 2)]).then_inc(w_in[u], 16)
            sp.dma_start(slots.rearrange("(n p) c -> p n c", p=ST_), empty.unsqueeze(1).to_broadcast([ST_, NS, ROW])).then_inc(empty_in, 16)
            sp.wait_ge(h2_done, DONE(NT - 1))
            sp.dma_start(out[0:(NT - 1) * TT, :].rearrange("(t p) c -> p t c", p=TT),
                         H[:, 0:(NT - 1) * C].rearrange("p (t c) -> p t c", c=C)).then_inc(h_stored, 16)
            sp.dma_start(out[(NT - 1) * TT:B * T, :], H[0:LAST, (NT - 1) * C:NT * C]).then_inc(h_stored, 16)
            sp.dma_start(out[B * T:B * T + DUMP, :], empty[:, 0:C]).then_inc(h_stored, 16)
            sp.wait_ge(s_mm, DONE(NT - 1))
            for dst, src in LATER:
                sp.dma_start(dst, src).then_inc(later_in, 16)
            sp.wait_ge(dispatched, 16 * TOPK * NT)
            sp.wait_ge(empty_in, 16)

            def load_rows(s, u, free):
                at = ds(s * ST_, ST_)
                if free:
                    sp.wait_ge(xr_mm, FREE2(s))
                sp.dma_start(XR[u], slots[at, 0:C]).then_inc(rows_in[u], 16)
                if free:
                    sp.wait_ge(gate_done, FREE2(s))
                sp.dma_start(XM[u], slots[at, C:ROW]).then_inc(meta_in[u], 16)

            load_rows(0, 0, False)
            load_rows(1, 1, False)
            with sp.Fori(0, (NS - 3) // 2) as i:
                for u in range(2):
                    load_rows(i * 2 + (2 + u), u, True)
            load_rows(NS - 1, 0, True)
            sp.wait_ge(h_stored, 48)
            sp.wait_ge(y_added, ADDED(NS))

        @block.gpsimd
        def _(gp):
            for s in (kbl_done, yl_done):
                gp.sem_inc(s, CR)
            fills = [(EPSV[:, :], EPS / S_X ** 2), (ONE[:, :], S_G), (SCALE[:, :], S_W), (XN[HC:HC + 1, :], 0.0),
                     (XN[HC:HC + 1, :].rearrange("p (t c) -> p t c", t=NT)[:, :, 0:2 * TT], S_X),
                     (YT[HC:HC + 1, :], 0.0), (YT[HC:HC + 1, :].rearrange("p (t c) -> p t c", t=2)[:, :, 0:2 * ST_], S_X)]
            fills += [(buf[p][:, :], 0.0) for buf in (QM, VB) for p in range(2)]
            for n, (dst, value) in enumerate(fills):
                if n:
                    gp.wait_ge(consts_set, n)
                nc.gpsimd.memset(dst, value).then_inc(consts_set, 1)
            gp.wait_ge(consts_set, len(fills))
            gp.wait_ge(const_in, 16 * len(CONSTS))
            nc.gpsimd.tensor_copy(VB[0][:, :].rearrange("p (n c) -> p n c", c=VC)[:, :, GC:VC],
                                  VO[:, :].unsqueeze(1).to_broadcast([KEYS, 2 * TI * NG, GH])).then_inc(consts_set, 1)
            gp.wait_ge(consts_set, FILLS)
            gp.wait_ge(small_lo, len(SMALL))
            nc.gpsimd.memset(PTR[:, :], 0.0).then_inc(pt_zero, 1)

            gp.sem_inc(w_lo, 2)

            def piece_low(n, u, to, at, raw):
                gp.wait_ge(w_hi, n + 1)
                nc.gpsimd.tensor_tensor(to[1][0:raw.shape[0], ds(at, raw.shape[1])], raw,
                                        to[0][0:raw.shape[0], ds(at, raw.shape[1])], ALU.subtract).then_inc(w_lo, 1)

            def keys_low(t, u):
                gp.wait_ge(kl_done, DONE(t))
                gp.wait_ge(s_mm, FREE2(t))
                nc.gpsimd.tensor_tensor(
                    kbd(1, u).rearrange("p (c h k) -> p c h k", c=2, h=HH),
                    KP[1][:, u * 2 * TT:(u + 1) * 2 * TT].rearrange("p (c k) -> p c k", c=2).unsqueeze(2).to_broadcast([HC, 2, HH, TT]),
                    HM[:, :].rearrange("p (h k) -> p h k", h=HH).unsqueeze(1).to_broadcast([HC, 2, HH, TT]),
                    ALU.mult).then_inc(kbl_done, 1)

            def y_low(t, u):
                gp.wait_ge(yh_done, t + 1)
                nc.gpsimd.tensor_tensor(Y[1][:, ds(t * C, C)], YF[:, u * C:(u + 1) * C], Y[0][:, ds(t * C, C)], ALU.subtract).then_inc(yl_done, 1)

            with gp.Fori(0, N1_STEPS) as i:
                for u in range(2):
                    w1_piece(piece_low, i, u)
            keys_low(0, 0)
            keys_low(1, 1)
            keys_low(2, 0)
            with gp.Fori(0, W1_STEPS) as i:
                for u in range(2):
                    t = i * 2 + (1 + u)
                    y_low(t - 1, u)
                    keys_low(t + 2, 1 - u)
                    w1_piece(piece_low, i + N1_STEPS, u)
            with gp.Fori(0, W2_STEPS) as i:
                for u in range(2):
                    t = i * 2 + (2 * W1_STEPS + 1 + u)
                    y_low(t - 1, u)
                    keys_low(t + 2, 1 - u)
                    w2_piece(piece_low, i, u)
            y_low(NT - 4, 0)
            keys_low(NT - 1, 1)
            y_low(NT - 3, 1)
            y_low(NT - 2, 0)
            y_low(NT - 1, 1)
            with gp.Fori(0, OP_STEPS) as i:
                for u in range(2):
                    w2_piece(piece_low, i + W2_STEPS, u)
            gp.wait_ge(s_mm, DONE(NT - 1))
            nc.gpsimd.memset(ONES, 1.0).then_inc(ones_set, 1)
            gp.wait_ge(ones_set, 1)
            nc.gpsimd.memset(CUM[0], 0.0).then_inc(ones_set, 1)
            gp.wait_ge(ones_set, 2)
            nc.gpsimd.memset(CUM[1], 0.0).then_inc(ones_set, 1)
            gp.wait_ge(empty_in, 16)
            gp.wait_ge(route, ROUTED)
            for t in range(NT):
                n = TT if t < NT - 1 else LAST
                for k in range(TOPK):
                    gp.indirect_dma_start(out=slots, out_offset=bass.IndirectOffsetOnAxis(ap=SLOTI[0:n, k * NT + t:k * NT + t + 1], axis=0),
                                          in_=RB[0:n, t * ROW:(t + 1) * ROW], in_offset=None).then_inc(dispatched, 16)
            gp.wait_ge(h_stored, 48)

            def add_rows(s, u, first=False):
                if not first:
                    gp.wait_ge(add_turn, s)
                    gp.wait_ge(y_added, ADDED(s))
                gp.wait_ge(y_done, DONE(s))
                nc.gpsimd.tensor_tensor(JUNK[0:1, :], CUM[0][0:1, 0:1], CUM[0][0:1, 0:1], ALU.add).then_inc(add_turn, 1)
                gp.indirect_dma_start(out=out, out_offset=bass.IndirectOffsetOnAxis(ap=IDX[u], axis=0),
                                      in_=YO[u], in_offset=None, compute_op=ALU.add).then_inc(y_added, 16)

            add_rows(0, 0, True)
            with gp.Fori(0, (NS - 1) // 2) as i:
                for v in (1, 2):
                    add_rows(i * 2 + v, v % 2)

        @block.scalar
        def _(act):
            for s in (xh_done, h_done, N1[1], N1[4], qh_done, kh_done, vh_done, p_done, pth_done, yt_done, N2[1], N2[4], gelu_done, gh_done):
                act.sem_inc(s, CR)
            for n, (_, parts, _, _) in enumerate(SMALL):
                act.wait_ge(raw_in[n], 16)
                nc.scalar.activation(parts[0][:, :], RAW[n], ACT.Copy, scale=S_W).then_inc(small_hi, 1)

            def patch_hi(t, u, slot, k, landed):
                act.wait_ge(x_in[slot], landed)
                act.wait_ge(emb_mm, FREE2(t))
                nc.scalar.activation(xhl(u, 0), xs(slot, k), ACT.Copy, scale=S_X).then_inc(xh_done, 1)

            def h_out(t, u):
                act.wait_ge(emb_mm, DONE(t))
                nc.scalar.activation(htile(t), bank(u, TT, C), ACT.Copy, scale=1 / S_XW).then_inc(h_done, 1)

            patch_hi(0, 0, 0, 0, 16)
            with act.Fori(0, (NT - 2) // 4) as i:
                for v in range(4):
                    t, ahead = i * 4 + v, v + 1
                    patch_hi(t + 1, ahead % 2, ahead // 2 % 2, ahead % 2, i * 16 + (16 if ahead < 4 else 32))
                    h_out(t, v % 2)
            patch_hi(NT - 1, 1, 0, 1, 16 * (NT // 4 + 1))
            h_out(NT - 2, 0)
            h_out(NT - 1, 1)

            def deviation(mv, done):
                act.wait_ge(mv, 6)
                nc.scalar.activation(RS[:, :], VAR[:, :], ACT.Sqrt, bias=EPSV[:, 0:1], scale=1 / (C * S_X ** 2)).then_inc(done, 1)

            def norm_hi(N, t, u):
                act.wait_ge(N[0], DONE(t))
                act.wait_ge(N[3], FREE2(t))
                nc.scalar.activation(row_part(N, t, u, 0, C), XF[:, u * C:(u + 1) * C], ACT.Copy).then_inc(N[1], 1)

            def norm_out(N, t, u):
                act.wait_ge(N[3], DONE(t))
                if N is N1:
                    nc.scalar.activation(XN[0:HC, ds(t * (4 * TT), 4 * TT)], bank(2 + u, HC, 4 * TT, F16), ACT.Copy).then_inc(N[4], 1)
                else:
                    act.wait_ge(r_mm, FREE2(t))
                    nc.scalar.activation(YT[0:HC, u * 4 * ST_:(u + 1) * 4 * ST_].rearrange("p (n q) -> p n q", q=ST_)[:, :, 0:TT],
                                         bank(2 + u, HC, 4 * TT, F16).rearrange("p (n q) -> p n q", q=TT), ACT.Copy).then_inc(N[4], 1)

            def piece_hi(n, u, to, at, raw):
                act.wait_ge(w_in[u], (n - u) * 8 + 16)
                nc.scalar.activation(raw, raw, ACT.Copy, scale=S_W).then_inc(w_scaled, 1)
                act.wait_ge(w_scaled, n + 1)
                nc.scalar.activation(to[0][0:raw.shape[0], ds(at, raw.shape[1])], raw, ACT.Copy).then_inc(w_hi, 1)

            def norm(N, pieces):
                norm_hi(N, 0, 0)
                with act.Fori(0, N1_STEPS) as i:
                    for v in range(4):
                        norm_hi(N, i * 4 + (v + 1), (v + 1) % 2)
                        norm_out(N, i * 4 + v, v % 2)
                        if pieces and v % 2:
                            w1_piece(piece_hi, i, v // 2)
                norm_hi(N, NT - 1, 1)
                norm_out(N, NT - 2, 0)
                norm_out(N, NT - 1, 1)

            act.wait_ge(consts_set, 1)
            deviation(mv_done, sd_done)
            norm(N1, True)

            def qkv_hi(t, u):
                act.wait_ge(qk_mm, DONE(t))
                act.wait_ge(s_mm, FREE2(t))
                qk = bank(0, HC, 4 * TT)
                nc.scalar.activation(diag(QM[0], u, 2), qk[:, 0:2 * TT].rearrange("p (b q) -> p b q", q=T), ACT.Copy,
                                     scale=S_Q / S_XW).then_inc(qh_done, 1)
                act.wait_ge(kbh_done, FREE2(t))
                act.wait_ge(kbl_done, FREE2(t))
                nc.scalar.activation(KP[0][:, u * 2 * TT:(u + 1) * 2 * TT], qk[:, 2 * TT:4 * TT], ACT.Copy,
                                     scale=S_Q / S_XW).then_inc(kh_done, 1)
                act.wait_ge(v_mm, DONE(t))
                act.wait_ge(vr_mm, FREE2(t))
                nc.scalar.activation(VP[0][:, u * C:(u + 1) * C], bank(1, TT, C), ACT.Copy, scale=S_V / S_XW).then_inc(vh_done, 1)

            def exps(t, u):
                act.wait_ge(sub_done, DONE(t))
                pr = PR[:, u * HEADS * T:(u + 1) * HEADS * T]
                nc.scalar.activation(pr, pr, ACT.Exp, scale=HD ** -0.5 / S_Q ** 2).then_inc(p_done, 1)

            def y_hi(t, u):
                act.wait_ge(yf_done, DONE(t))
                nc.scalar.activation(Y[0][:, ds(t * C, C)], YF[:, u * C:(u + 1) * C], ACT.Copy).then_inc(yh_done, 1)

            def probs_hi(t, u):
                act.wait_ge(pt_mm, DONE(t))
                act.wait_ge(o_mm, FREE2(t))
                nc.scalar.activation(diag(PT[0], u, NG), bank(3, KEYS, NG * TT).rearrange("p (b q) -> p b q", q=T), ACT.Copy,
                                     scale=S_P).then_inc(pth_done, 1)

            act.wait_ge(consts_set, FILLS)
            act.wait_ge(pt_zero, 1)
            qkv_hi(0, 0)
            qkv_hi(1, 1)
            exps(0, 0)
            qkv_hi(2, 0)
            probs_hi(0, 0)
            with act.Fori(0, W1_STEPS) as i:
                for u in range(2):
                    t = i * 2 + (1 + u)
                    exps(t, 1 - u)
                    y_hi(t - 1, u)
                    qkv_hi(t + 2, 1 - u)
                    probs_hi(t, 1 - u)
                    w1_piece(piece_hi, i + N1_STEPS, u)
            with act.Fori(0, W2_STEPS) as i:
                for u in range(2):
                    t = i * 2 + (2 * W1_STEPS + 1 + u)
                    exps(t, 1 - u)
                    y_hi(t - 1, u)
                    qkv_hi(t + 2, 1 - u)
                    probs_hi(t, 1 - u)
                    w2_piece(piece_hi, i, u)
            exps(NT - 3, 1)
            y_hi(NT - 4, 0)
            qkv_hi(NT - 1, 1)
            probs_hi(NT - 3, 1)
            for t in (NT - 2, NT - 1):
                exps(t, t % 2)
                y_hi(t - 1, 1 - t % 2)
                probs_hi(t, t % 2)
            y_hi(NT - 1, 1)

            act.wait_ge(consts_set, FILLS)
            def y_out(t, u):
                    act.wait_ge(yt_mm, DONE(t))
                    act.wait_ge(op_mm, FREE2(t))
                    nc.scalar.activation(YT[0:HC, u * 4 * ST_:(u + 1) * 4 * ST_].rearrange("p (n q) -> p n q", q=ST_)[:, :, 0:TT],
                                         bank(u, HC, 4 * TT, F16).rearrange("p (n q) -> p n q", q=TT), ACT.Copy).then_inc(yt_done, 1)
            with act.Fori(0, OP_STEPS) as i:
                for v in range(4):
                    y_out(i * 4 + v, v % 2)
                    if v % 2:
                        w2_piece(piece_hi, i + W2_STEPS, v // 2)
            with act.Fori(0, (NT - 4 * OP_STEPS) // 4) as i:
                for v in range(4):
                    y_out(i * 4 + (4 * OP_STEPS + v), v % 2)
            for t in range(NT // 4 * 4, NT):
                y_out(t, t % 2)
            deviation(mv2_done, sd2_done)
            norm(N2, False)
            act.wait_ge(route, 3)
            nc.scalar.activation(RT[:, NT:2 * NT], RT[:, 0:NT], ACT.Exp, scale=1 / S_XW).then_inc(gap_exp, 1)
            nc.scalar.activation(JUNK2, EPSV[0:1, :], ACT.Gelu).then_inc(gap_exp, 1)

            def hidden(s, u):
                g = G[:, u * F:(u + 1) * F]
                act.wait_ge(up_mm, DONE(s))
                act.wait_ge(gl_done, FREE2(s))
                nc.scalar.activation(g.rearrange("p (h c) -> p h c", h=2),
                                     PSA[:, 2 * u * 512:(2 * u + 2) * 512].rearrange("p (h c) -> p h c", h=2)[:, :, 0:F // 2],
                                     ACT.Gelu, scale=1 / S_XW).then_inc(gelu_done, 1)
                act.wait_ge(gelu_done, DONE(s))
                act.wait_ge(down_mm, FREE2(s))
                nc.scalar.activation(GP[0][:, u * F:(u + 1) * F], g, ACT.Copy, scale=S_G).then_inc(gh_done, 1)

            with act.Fori(0, (NS - 1) // 6) as i:
                for v in range(6):
                    hidden(i * 6 + v, v % 2)
            hidden(NS - 1, 0)

        @block.vector
        def _(dve):
            for s in (xl_done, st_done, N1[0], N1[2], ql_done, kl_done, vl_done, kbh_done, mx_done, sub_done,
                      ptl_done, vbl_done, rd_done, yf_done, h2_done, st2_done, N2[0], N2[2], lg_done, gl_done, gate_done, xt_done, y_done):
                dve.sem_inc(s, CR)

            def low(dst, src, scale, hi):
                return nc.vector.scalar_tensor_tensor(dst, src, scale, hi, ALU.mult, ALU.subtract)

            for n, (_, parts, _, _) in enumerate(SMALL):
                dve.wait_ge(small_hi, n + 1)
                low(parts[1][:, :], RAW[n], S_W, parts[0][:, :]).then_inc(small_lo, 1)

            def patch_lo(t, u, slot, k):
                dve.wait_ge(xh_done, DONE(t))
                low(xhl(u, 1), xs(slot, k), S_X, xhl(u, 0)).then_inc(xl_done, 1)

            def stats(t, st):
                nc.vector.bn_stats(ST[:, ds(t * 6, 6)], htile(t)).then_inc(st, 1)

            def variances(st, mv):
                s = ST[:, :].rearrange("p (t c) -> p t c", c=6)
                dve.wait_ge(st, DONE(NT - 1))
                nc.vector.tensor_tensor(MEAN[:, :], s[:, :, 1], s[:, :, 4], ALU.add).then_inc(mv, 1)
                nc.vector.tensor_tensor(DM[:, :], s[:, :, 1], s[:, :, 4], ALU.subtract).then_inc(mv, 1)
                nc.vector.tensor_tensor(VAR[:, :], s[:, :, 2], s[:, :, 5], ALU.add).then_inc(mv, 1)
                dve.wait_ge(mv, 3)
                nc.vector.tensor_scalar(MEAN[:, :], MEAN[:, :], 0.5, None, ALU.mult).then_inc(mv, 1)
                nc.vector.scalar_tensor_tensor(DM[:, :], DM[:, :], 0.25 * C, DM[:, :], ALU.mult, ALU.mult).then_inc(mv, 1)
                dve.wait_ge(mv, 5)
                nc.vector.tensor_tensor(VAR[:, :], VAR[:, :], DM[:, :], ALU.add).then_inc(mv, 1)

            patch_lo(0, 0, 0, 0)
            patch_lo(1, 1, 0, 1)
            with dve.Fori(0, (NT - 2) // 4) as i:
                for v in range(4):
                    t, ahead = i * 4 + (1 + v), v + 2
                    dve.wait_ge(h_done, DONE(t - 1))
                    patch_lo(t + 1, ahead % 2, ahead // 2 % 2, ahead % 2)
                    stats(t - 1, st_done)
            dve.wait_ge(h_done, DONE(NT - 1))
            stats(NT - 2, st_done)
            stats(NT - 1, st_done)
            variances(st_done, mv_done)

            def norm_row(N, t, u):
                dve.wait_ge(N[2], FREE2(t))
                nc.vector.tensor_scalar(XF[:, u * C:(u + 1) * C], htile(t), MEAN[:, ds(t, 1)], RS[:, ds(t, 1)],
                                        ALU.subtract, ALU.mult).then_inc(N[0], 1)

            def norm_lo(N, t, u):
                dve.wait_ge(N[1], DONE(t))
                nc.vector.tensor_tensor(row_part(N, t, u, C, C), XF[:, u * C:(u + 1) * C],
                                        row_part(N, t, u, 0, C), ALU.subtract).then_inc(N[2], 1)

            def norm(N, sd, rs):
                dve.wait_ge(sd, 1)
                nc.vector.reciprocal(RS[:, :], RS[:, :]).then_inc(rs, 1)
                dve.wait_ge(rs, 1)
                norm_row(N, 0, 0)

            norm(N1, sd_done, rs_done)
            with dve.Fori(0, (NT - 2) // 4) as i:
                for v in range(4):
                    norm_row(N1, i * 4 + (v + 1), (v + 1) % 2)
                    norm_lo(N1, i * 4 + v, v % 2)
            norm_row(N1, NT - 1, 1)
            norm_lo(N1, NT - 2, 0)
            norm_lo(N1, NT - 1, 1)

            def qkv_lo(t, u):
                dve.wait_ge(qh_done, DONE(t))
                dve.wait_ge(kh_done, DONE(t))
                qk = bank(0, HC, 4 * TT)
                low(diag(QM[1], u, 2), qk[:, 0:2 * TT].rearrange("p (b q) -> p b q", q=T), S_Q / S_XW, diag(QM[0], u, 2)).then_inc(ql_done, 1)
                kp = [KP[p][:, u * 2 * TT:(u + 1) * 2 * TT] for p in range(2)]
                low(kp[1], qk[:, 2 * TT:4 * TT], S_Q / S_XW, kp[0]).then_inc(kl_done, 1)
                dve.wait_ge(vh_done, DONE(t))
                low(VP[1][:, u * C:(u + 1) * C], bank(1, TT, C), S_V / S_XW, VP[0][:, u * C:(u + 1) * C]).then_inc(vl_done, 1)
                dve.wait_ge(s_mm, FREE2(t))
                nc.vector.tensor_tensor(
                    kbd(0, u).rearrange("p (c h k) -> p c h k", c=2, h=HH),
                    kp[0].rearrange("p (c k) -> p c k", c=2).unsqueeze(2).to_broadcast([HC, 2, HH, TT]),
                    HM[:, :].rearrange("p (h k) -> p h k", h=HH).unsqueeze(1).to_broadcast([HC, 2, HH, TT]),
                    ALU.mult).then_inc(kbh_done, 1)

            def shift(t, u):
                dve.wait_ge(s_mm, DONE(t))
                dve.wait_ge(sub_done, FREE2(t))
                mx = MX[:, u * HEADS:(u + 1) * HEADS]
                nc.vector.tensor_reduce(mx, heads(bank(2, TT, HEADS * T)), AX.X, ALU.max).then_inc(mx_done, 1)
                dve.wait_ge(mx_done, DONE(t))
                dve.wait_ge(pt_mm, FREE2(t))
                nc.vector.tensor_tensor(heads(PR[:, u * HEADS * T:(u + 1) * HEADS * T]), heads(bank(2, TT, HEADS * T)),
                                        mx.unsqueeze(2).to_broadcast([TT, HEADS, T]), ALU.subtract).then_inc(sub_done, 1)

            def values(t, u):
                dve.wait_ge(vr_mm, DONE(t))
                dve.wait_ge(o_mm, FREE2(t))
                for p, done in ((0, vbh_done), (1, vbl_done)):
                    nc.vector.tensor_tensor(
                        vbd(p, u).rearrange("p (b g c) -> p b g c", b=TI, g=NG)[:, :, :, 0:GC],
                        PSA[0:KEYS, 4 * 512:7 * 512].rearrange("p (b c) -> p b c", b=TI)[:, :, p * C:(p + 1) * C].rearrange("p b (g c) -> p b g c", g=NG),
                        VM[:, :].rearrange("p (g c) -> p g c", g=NG).unsqueeze(1).to_broadcast([KEYS, TI, NG, GC]),
                        ALU.mult).then_inc(done, 1)

            def probs_lo(t, u):
                dve.wait_ge(pth_done, DONE(t))
                low(diag(PT[1], u, NG), bank(3, KEYS, NG * TT).rearrange("p (b q) -> p b q", q=T), S_P, diag(PT[0], u, NG)).then_inc(ptl_done, 1)

            def outputs(t, u):
                dve.wait_ge(o_mm, DONE(t))
                o = bank(7, TT, NG * VC).rearrange("p (g c) -> p g c", g=NG)
                rd = RD[:, u * HEADS:(u + 1) * HEADS].rearrange("p (g h) -> p g h", g=NG)
                dve.wait_ge(yf_done, FREE2(t))
                nc.vector.reciprocal(rd, o[:, :, GC:VC]).then_inc(rd_done, 1)
                dve.wait_ge(rd_done, DONE(t))
                dve.wait_ge(yl_done, FREE2(t))
                nc.vector.tensor_tensor(
                    YF[:, u * C:(u + 1) * C].rearrange("p (g h d) -> p g h d", g=NG, h=GH),
                    o[:, :, 0:GC].rearrange("p g (h d) -> p g h d", h=GH),
                    rd.unsqueeze(3).to_broadcast([TT, NG, GH, HD]), ALU.mult).then_inc(yf_done, 1)

            dve.wait_ge(const_in, 16 * len(CONSTS))
            dve.wait_ge(consts_set, FILLS)
            qkv_lo(0, 0)
            qkv_lo(1, 1)
            shift(0, 0)
            values(0, 0)
            qkv_lo(2, 0)
            probs_lo(0, 0)
            with dve.Fori(0, (NT - 4) // 2) as i:
                for u in range(2):
                    t = i * 2 + (1 + u)
                    shift(t, 1 - u)
                    outputs(t - 1, u)
                    values(t, 1 - u)
                    qkv_lo(t + 2, 1 - u)
                    probs_lo(t, 1 - u)
            shift(NT - 3, 1)
            outputs(NT - 4, 0)
            values(NT - 3, 1)
            qkv_lo(NT - 1, 1)
            probs_lo(NT - 3, 1)
            shift(NT - 2, 0)
            outputs(NT - 3, 1)
            values(NT - 2, 0)
            probs_lo(NT - 2, 0)
            shift(NT - 1, 1)
            outputs(NT - 2, 0)
            values(NT - 1, 1)
            probs_lo(NT - 1, 1)
            outputs(NT - 1, 1)

            def residual(t, u):
                dve.wait_ge(op_mm, DONE(t))
                nc.vector.scalar_tensor_tensor(htile(t), bank(2 + u, TT, C), 1 / S_XW, htile(t), ALU.mult, ALU.add).then_inc(h2_done, 1)

            residual(0, 0)
            with dve.Fori(0, (NT - 2) // 4) as i:
                for v in range(4):
                    t = i * 4 + (1 + v)
                    dve.wait_ge(h2_done, DONE(t - 1))
                    residual(t, (1 + v) % 2)
                    stats(t - 1, st2_done)
            dve.wait_ge(h2_done, DONE(NT - 2))
            residual(NT - 1, 1)
            stats(NT - 2, st2_done)
            dve.wait_ge(h2_done, DONE(NT - 1))
            stats(NT - 1, st2_done)
            variances(st2_done, mv2_done)
            norm(N2, sd2_done, rs2_done)

            def logits(t, u):
                dve.wait_ge(r_mm, DONE(t))
                nc.vector.tensor_copy(LG[:, ds(t * E, E)], bank(4 + u, TT, E)).then_inc(lg_done, 1)

            norm_row(N2, 1, 1)
            norm_lo(N2, 0, 0)
            norm_row(N2, 2, 0)
            norm_lo(N2, 1, 1)
            with dve.Fori(0, (NT - 4) // 6) as i:
                for v in range(6):
                    t = i * 6 + (2 + v)
                    norm_row(N2, t + 1, (v + 1) % 2)
                    norm_lo(N2, t, v % 2)
                    logits(t - 2, v % 2)
            norm_row(N2, NT - 1, 1)
            norm_lo(N2, NT - 2, 0)
            logits(NT - 4, 0)
            norm_lo(N2, NT - 1, 1)
            logits(NT - 3, 1)
            logits(NT - 2, 0)
            logits(NT - 1, 1)

            dve.wait_ge(lg_done, DONE(NT - 1))
            dve.wait_ge(pt_mm, DONE(NT - 1))
            dve.wait_ge(w_lo, 2 * PIECES + 2)
            for t in range(NT):
                nc.vector.max(M8[:, t * E:(t + 1) * E], LG[:, t * E:(t + 1) * E]).then_inc(mx_done, 1)
            for t in range(NT):
                dve.wait_ge(mx_done, t + NT + 1 + CR)
                nc.vector.max_index(I8[:, t * E:(t + 1) * E], M8[:, t * E:(t + 1) * E], LG[:, t * E:(t + 1) * E]).then_inc(lg_done, 1)
            dve.wait_ge(lg_done, 2 * NT + CR)
            m8 = M8.rearrange("p (t e) -> p t e", e=E)
            i8 = I8.rearrange("p (t e) -> p t e", e=E)
            col = [RT[:, n * NT:(n + 1) * NT] for n in range(8)]
            nc.vector.tensor_tensor(col[0], m8[:, :, 1], m8[:, :, 0], ALU.subtract).then_inc(route, 1)
            for k in range(2):
                nc.vector.tensor_copy(col[2 + k], i8[:, :, k]).then_inc(route, 1)
            dve.wait_ge(route, 3)
            for k in range(2):
                nc.vector.tensor_tensor(OH[k].rearrange("p (t e) -> p t e", e=E), EID[:, :].unsqueeze(1).to_broadcast([TT, NT, E]),
                                        col[2 + k].unsqueeze(2).to_broadcast([TT, NT, E]), ALU.is_equal).then_inc(route, 1)
            def routed(n):
                dve.wait_ge(route, n)

            own3 = [OH[k].rearrange("p (t e) -> p t e", e=E) for k in range(2)]
            routed(5)
            dve.wait_ge(later_in, 16 * len(LATER))
            nc.vector.tensor_tensor(CHOSEN, OH[0], OH[1], ALU.add).then_inc(route, 1)
            routed(6)
            last = CHOSEN[:, (NT - 1) * E:NT * E]
            nc.vector.tensor_scalar(last, last, REAL[:, 0:1], None, ALU.mult).then_inc(route, 1)
            carry = RB.rearrange("p (t c) -> p t c", c=ROW)
            dve.wait_ge(gap_exp, 1)
            nc.vector.tensor_scalar(col[4], col[1], 1.0, S_G * S_W, ALU.add, ALU.mult).then_inc(route, 1)
            routed(8)
            nc.vector.reciprocal(col[4], col[4]).then_inc(route, 1)
            routed(9)
            nc.vector.tensor_tensor(col[5], col[4], col[1], ALU.mult).then_inc(route, 1)
            routed(10)
            nc.vector.tensor_tensor(carry[:, :, GAP], col[4], col[5], ALU.subtract).then_inc(route, 1)
            nc.vector.tensor_copy(carry[:, :, SECOND], col[5]).then_inc(route, 1)
            nc.vector.tensor_copy(carry[:, :, FIRST], col[2]).then_inc(route, 1)
            nc.vector.tensor_copy(carry[:, :, TOKEN], TOKENS).then_inc(route, 1)
            dve.wait_ge(rank_mm, 1)
            dve.wait_ge(ones_set, 3)
            nc.vector.tensor_scalar(CNTI, bank(7, ST_, E), float(ST_ - 1), None, ALU.add).then_inc(count, 1)
            dve.wait_ge(count, 1)
            nc.vector.tensor_scalar(CNTI, CNTI, 7, None, ALU.logical_shift_right).then_inc(count, 1)
            dve.wait_ge(count, 2)
            nc.vector.tensor_copy(CUM[0][:, E:2 * E], CNTI).then_inc(count, 1)
            for n, d in enumerate((1, 2, 4)):
                dve.wait_ge(count, 3 + n)
                a = CUM[n % 2]
                nc.vector.tensor_tensor(CUM[1 - n % 2][:, E:2 * E], a[:, E:2 * E], a[:, E - d:2 * E - d], ALU.add).then_inc(count, 1)
            dve.wait_ge(count, 6)
            cum = CUM[1]
            nc.vector.tensor_scalar(START, cum[:, E - 1:2 * E - 1], float(ST_), None, ALU.mult).then_inc(count, 1)
            passed = PASSED.rearrange("p (s e) -> p s e", e=E - 1)
            nc.vector.tensor_tensor(passed, TILENO.unsqueeze(2).to_broadcast([ST_, NS, E - 1]),
                                    cum[:, E:2 * E - 1].unsqueeze(1).to_broadcast([ST_, NS, E - 1]), ALU.is_ge).then_inc(count, 1)
            dve.wait_ge(count, 7)
            nc.vector.tensor_tensor(SLOTS.rearrange("p (t e) -> p t e", e=E), bank(6, TT, NT * E).rearrange("p (t e) -> p t e", e=E),
                                    START[0:TT].unsqueeze(1).to_broadcast([TT, NT, E]), ALU.add).then_inc(count, 1)
            dve.wait_ge(count, 9)
            nc.vector.tensor_reduce(EXPF, passed, AX.X, ALU.add).then_inc(count, 1)
            for k in range(2):
                nc.vector.tensor_tensor(OWN[k], OH[k], SLOTS, ALU.mult).then_inc(count, 1)
            for k in range(2):
                dve.wait_ge(count, 11 + k)
                nc.vector.tensor_reduce(col[6 + k], OWN[k].rearrange("p (t e) -> p t e", e=E), AX.X, ALU.add).then_inc(count, 1)
            dve.wait_ge(count, 14)
            nc.vector.tensor_copy(SLOTI, RT[:, 6 * NT:8 * NT]).then_inc(route, 1)
            nc.vector.tensor_copy(EXPI, EXPF).then_inc(count, 1)

            def rows_out(s, u):
                dve.wait_ge(xr_mm, DONE(s))
                dve.wait_ge(up_mm, FREE2(s))
                nc.vector.tensor_copy(YT[0:HC, u * 4 * ST_:(u + 1) * 4 * ST_], bank(6 + u, HC, 4 * ST_, F16)).then_inc(xt_done, 1)

            def hidden_lo(s, u):
                dve.wait_ge(gh_done, DONE(s))
                g = slice(u * F, (u + 1) * F)
                low(GP[1][:, g], G[:, g], S_G, GP[0][:, g]).then_inc(gl_done, 1)

            def gates(s, u, landed, waits=True):
                dve.wait_ge(meta_in[u], landed)
                if waits:
                    dve.wait_ge(y_added, ADDED(s - 1))
                dve.wait_ge(y_done, FREE2(s))
                nc.vector.tensor_tensor(MATCH[u], XM[u][:, 1:2], EXPF[:, ds(s, 1)], ALU.is_equal).then_inc(match_done, 1)
                nc.vector.tensor_copy(IDX[u], XM[u][:, 0:1]).then_inc(match_done, 1)
                dve.wait_ge(match_done, 2 * s + 2)
                nc.vector.scalar_tensor_tensor(GATE[u], MATCH[u], XM[u][:, 2:3], XM[u][:, 3:4], ALU.mult, ALU.add).then_inc(gate_done, 1)

            def gated(s, u):
                dve.wait_ge(down_mm, DONE(s))
                dve.wait_ge(gate_done, DONE(s))
                nc.vector.tensor_scalar(YO[u], bank(4 + u, ST_, C), GATE[u][:, 0:1], None, ALU.mult).then_inc(y_done, 1)

            dve.wait_ge(count, 15)
            rows_out(0, 0)
            gates(0, 0, 16, False)
            rows_out(1, 1)
            hidden_lo(0, 0)

            def step(s, u, landed, waits=True):
                rows_out(s + 2, u)
                hidden_lo(s + 1, 1 - u)
                gated(s, u)
                gates(s + 1, 1 - u, landed, waits)

            step(0, 0, 16, False)
            with dve.Fori(0, (NS - 3) // 2) as i:
                for v in (1, 2):
                    step(i * 2 + v, v % 2, i * 16 + 32)
            hidden_lo(NS - 1, 0)
            gated(NS - 2, 1)
            gates(NS - 1, 0, 16 * (NS // 2 + 1))
            gated(NS - 1, 0)

        @block.tensor
        def _(pe):
            for s in (emb_mm, N1[3], qk_mm, v_mm, s_mm, pt_mm, vr_mm, o_mm, yt_mm, op_mm, N2[3], r_mm, up_mm, down_mm, xr_mm):
                pe.sem_inc(s, CR)

            def embed(t, u):
                pe.wait_ge(xl_done, DONE(t))
                pe.wait_ge(h_done, FREE2(t))
                n = 0
                for k in range(KT):
                    for a, b in PRODUCTS:
                        ins = nc.tensor.matmul(bank(u, TT, C), xhl(u, a)[:, k * TT:(k + 1) * TT], WT[b][:, k * C:(k + 1) * C],
                                               start=n == 0, stop=n == 3 * KT - 1)
                        n += 1
                ins.then_inc(emb_mm, 1)

            pe.wait_ge(small_lo, 1)
            with pe.Fori(0, NT // 2) as i:
                for u in range(2):
                    embed(i * 2 + u, u)

            def norm_transpose(N, t, u):
                pe.wait_ge(N[2], DONE(t))
                pe.wait_ge(N[4], FREE2(t))
                for p in range(2):
                    for c in range(2):
                        n = 2 * p + c
                        ins = nc.tensor.transpose(bank(2 + u, HC, 4 * TT, F16)[:, n * TT:(n + 1) * TT],
                                                  row_part(N, t, u, n * HC, HC), IDH[0:TT, 0:TT])
                ins.then_inc(N[3], 1)

            pe.wait_ge(const_in, 16 * len(CONSTS))
            with pe.Fori(0, NT // 2) as i:
                for u in range(2):
                    norm_transpose(N1, i * 2 + u, u)

            def qkv(t, u):
                pe.wait_ge(N1[4], DONE(t))
                pe.wait_ge(ql_done, FREE1(t))
                pe.wait_ge(kl_done, FREE1(t))
                for j in range(4):
                    n = 0
                    for c in range(2):
                        for a, b in PRODUCTS:
                            ins = nc.tensor.matmul(bank(0, 128, 4 * TT)[:, j * TT:(j + 1) * TT],
                                                   WA[a][:, c * 3 * C + j * HC:c * 3 * C + j * HC + 128], xn(t, b, c), start=n == 0, stop=n == 5)
                            n += 1
                ins.then_inc(qk_mm, 1)
                pe.wait_ge(vl_done, FREE1(t))
                n = 0
                for c in range(2):
                    for a, b in PRODUCTS:
                        ins = nc.tensor.matmul(bank(1, TT, C), xn(t, a, c), WA[b][:, c * 3 * C + 2 * C:(c + 1) * 3 * C], start=n == 0, stop=n == 5)
                        n += 1
                ins.then_inc(v_mm, 1)

            def scores(t, u):
                pe.wait_ge(ql_done, DONE(t))
                pe.wait_ge(kbh_done, DONE(t))
                pe.wait_ge(kbl_done, DONE(t))
                pe.wait_ge(sub_done, FREE1(t))
                nc.tensor.matmul(bank(2, TT, HEADS * T), SELQ[:, :], CAUS[:, :].unsqueeze(1).to_broadcast([T, HEADS, T]), start=True, stop=False)
                for c in range(2):
                    for b in range(TI):
                        for p, q in PRODUCTS:
                            at = (2 * u + c) * DW + b * TT
                            keys = kbd(q, u).rearrange("p (c h k) -> p c h k", c=2, h=HH)[:, c, :, b * T:(b + 1) * T]
                            ins = nc.tensor.matmul(bank(2, TT, HEADS * T)[:, c * HH * T:(c + 1) * HH * T], QM[p][:, at:at + TT], keys,
                                                   start=False, stop=(c, b, p) == (1, TI - 1, 1))
                ins.then_inc(s_mm, 1)

            def transpose_probs(t, u):
                pe.wait_ge(p_done, DONE(t))
                pe.wait_ge(ptl_done, FREE1(t))
                for g in range(NG):
                    at = u * HEADS * T + g * KEYS
                    ins = nc.tensor.transpose(bank(3, KEYS, NG * TT)[:, g * TT:(g + 1) * TT], PR[:, at:at + KEYS], IDF[0:TT, 0:TT])
                ins.then_inc(pt_mm, 1)

            def spread_values(t, u):
                pe.wait_ge(vl_done, DONE(t))
                pe.wait_ge(vbl_done, FREE1(t))
                for b in range(TI):
                    for p in range(2):
                        ins = nc.tensor.matmul(bank(4 + b, KEYS, 2 * C)[:, p * C:(p + 1) * C], SELV[:, b * KEYS:(b + 1) * KEYS],
                                               VP[p][:, u * C:(u + 1) * C], start=True, stop=True)
                ins.then_inc(vr_mm, 1)

            def outputs(t, u):
                pe.wait_ge(ptl_done, DONE(t))
                pe.wait_ge(vbl_done, DONE(t))
                pe.wait_ge(yf_done, FREE1(t))
                for g in range(NG):
                    n = 0
                    for b in range(TI):
                        for p, q in PRODUCTS:
                            at = (u * NG + g) * DW + b * TT
                            vat = (b * NG + g) * VC
                            ins = nc.tensor.matmul(bank(7, 128, NG * VC)[:, g * VC:(g + 1) * VC], PT[p][:, at:at + 128],
                                                   vbd(q, u)[:, vat:vat + VC], start=n == 0, stop=n == 3 * TI - 1)
                            n += 1
                ins.then_inc(o_mm, 1)

            pe.wait_ge(small_lo, len(SMALL))
            pe.wait_ge(consts_set, FILLS)
            pe.wait_ge(h_done, DONE(NT - 1))
            pe.wait_ge(N1[4], DONE(NT - 1))
            qkv(0, 0)
            qkv(1, 1)
            scores(0, 0)
            spread_values(0, 0)
            qkv(2, 0)
            transpose_probs(0, 0)
            with pe.Fori(0, (NT - 4) // 2) as i:
                for u in range(2):
                    t = i * 2 + (1 + u)
                    scores(t, 1 - u)
                    outputs(t - 1, u)
                    spread_values(t, 1 - u)
                    qkv(t + 2, 1 - u)
                    transpose_probs(t, 1 - u)
            scores(NT - 3, 1)
            outputs(NT - 4, 0)
            spread_values(NT - 3, 1)
            qkv(NT - 1, 1)
            transpose_probs(NT - 3, 1)
            scores(NT - 2, 0)
            outputs(NT - 3, 1)
            spread_values(NT - 2, 0)
            transpose_probs(NT - 2, 0)
            scores(NT - 1, 1)
            outputs(NT - 2, 0)
            spread_values(NT - 1, 1)
            transpose_probs(NT - 1, 1)
            outputs(NT - 1, 1)

            def transpose_y(t, u):
                pe.wait_ge(yl_done, DONE(t))
                pe.wait_ge(yt_done, FREE2(t))
                for p in range(2):
                    for c in range(2):
                        n = 2 * p + c
                        ins = nc.tensor.transpose(bank(u, HC, 4 * TT, F16)[:, n * TT:(n + 1) * TT], Y[p][:, ds(t * C + c * HC, HC)], IDH[0:TT, 0:TT])
                ins.then_inc(yt_mm, 1)

            def project(t, u):
                pe.wait_ge(yt_done, DONE(t))
                pe.wait_ge(h2_done, FREE2(t))
                n = 0
                for c in range(2):
                    for a, b in PRODUCTS:
                        at = u * 4 * ST_ + (2 * a + c) * ST_
                        ins = nc.tensor.matmul(bank(2 + u, TT, C), YT[:, at:at + TT], WO[b][:, c * C:(c + 1) * C], start=n == 0, stop=n == 5)
                        n += 1
                ins.then_inc(op_mm, 1)

            pe.wait_ge(ptl_done, DONE(NT - 1))
            pe.wait_ge(vl_done, DONE(NT - 1))
            transpose_y(0, 0)
            with pe.Fori(0, (NT - 2) // 4) as i:
                for v in range(4):
                    transpose_y(i * 4 + (v + 1), (v + 1) % 2)
                    project(i * 4 + v, v % 2)
            transpose_y(NT - 1, 1)
            project(NT - 2, 0)
            project(NT - 1, 1)

            def router(t, u):
                pe.wait_ge(N2[4], DONE(t))
                pe.wait_ge(lg_done, FREE2(t))
                n = 0
                for c in range(2):
                    for a, b in PRODUCTS:
                        at = u * 4 * ST_ + (2 * a + c) * ST_
                        ins = nc.tensor.matmul(bank(4 + u, TT, E), YT[0:HC, at:at + TT], WR[b][:, c * E:(c + 1) * E], start=n == 0, stop=n == 5)
                        n += 1
                ins.then_inc(r_mm, 1)

            pe.wait_ge(h2_done, DONE(NT - 1))
            norm_transpose(N2, 0, 0)
            with pe.Fori(0, (NT - 2) // 4) as i:
                for v in range(4):
                    norm_transpose(N2, i * 4 + (v + 1), (v + 1) % 2)
                    router(i * 4 + v, v % 2)
            norm_transpose(N2, NT - 1, 1)
            router(NT - 2, 0)
            router(NT - 1, 1)

            pe.wait_ge(route, 7)
            pe.wait_ge(ones_set, 1)
            pe.wait_ge(later_in, 16 * len(LATER))
            nc.tensor.matmul(bank(6, TT, NT * E), BEFORE[:, 0:TT], CHOSEN, start=True, stop=False)
            for d in range(1, NT):
                nc.tensor.matmul(bank(6, TT, NT * E)[:, d * E:NT * E], ONES[:, 0:TT], CHOSEN[:, 0:(NT - d) * E], start=False, stop=d == NT - 1)
            for t in range(NT):
                ins = nc.tensor.matmul(bank(7, ST_, E), ONES, CHOSEN[:, t * E:(t + 1) * E], start=t == 0, stop=t == NT - 1)
            ins.then_inc(rank_mm, 1)

            def transpose_rows(s, u, landed):
                pe.wait_ge(rows_in[u], landed)
                pe.wait_ge(xt_done, FREE2(s))
                x = XR[u].bitcast(F16)
                for n in range(4):
                    ins = nc.tensor.transpose(bank(6 + u, HC, 4 * ST_, F16)[:, n * ST_:(n + 1) * ST_], x[:, n * HC:(n + 1) * HC], IDH[:, :])
                ins.then_inc(xr_mm, 1)

            def up(s, u, e):
                pe.wait_ge(xt_done, DONE(s))
                pe.wait_ge(gelu_done, FREE2(s))
                for f in range(FC):
                    w = f % (FC // 2) * ST_
                    k = 0
                    for c in range(2):
                        for a, b in PRODUCTS:
                            at = u * 4 * ST_ + (2 * b + c) * ST_
                            ins = nc.tensor.matmul(bank(2 * u + f // (FC // 2), 128, FC // 2 * ST_)[:, w:w + ST_],
                                                   W1[a][:, ds(e * (2 * F) + (c * F + f * 128), 128)], YT[:, at:at + ST_], start=k == 0, stop=k == 5)
                            k += 1
                ins.then_inc(up_mm, 1)

            def down(s, u, e):
                pe.wait_ge(gl_done, DONE(s))
                pe.wait_ge(y_done, FREE2(s))
                for f in range(FC):
                    for a, b in PRODUCTS:
                        at = (u * FC + f) * ST_
                        nc.tensor.matmul(bank(4 + u, ST_, C), GP[a][:, at:at + ST_], W2[b][:, ds(e * W2E + f * C, C)],
                                         start=(f, a, b) == (0, 0, 0), stop=False)
                for p in range(2):
                    ins = nc.tensor.matmul(bank(4 + u, ST_, C), ONE[:, :], W2[p][0:1, ds(e * W2E + FC * C, C)], start=False, stop=p == 1)
                ins.then_inc(down_mm, 1)

            def experts(s, n):
                return nc.values_load_multi_w_load_instructions(EXPI[0:1, ds(s, n)], [mybir.EngineType.PE],
                                                                min_val=0, max_val=E - 1, 
                                                                skip_runtime_bounds_check_because="the table counts E - 1 comparisons")[1]

            pe.wait_ge(count, 15)
            pe.wait_ge(route, ROUTED)
            transpose_rows(0, 0, 16)
            transpose_rows(1, 1, 16)
            up(0, 0, experts(0, 1)[0])
            with pe.Fori(0, (NS - 3) // 8) as i:
                e = experts(i * 8, 9)
                for v in range(8):
                    s, u = i * 8 + v, v % 2
                    up(s + 1, 1 - u, e[v + 1])
                    transpose_rows(s + 2, u, i * 64 + 16 * (v // 2 + 2))
                    down(s, u, e[v])
            e = experts(NS - 3, 3)
            up(NS - 2, 1, e[1])
            transpose_rows(NS - 1, 0, 16 * (NS // 2 + 1))
            down(NS - 3, 0, e[0])
            up(NS - 1, 0, e[2])
            down(NS - 2, 1, e[1])
            down(NS - 1, 0, e[2])


def kernel(**inputs):
    import ml_dtypes
    import concourse.bacc as bacc
    from concourse.bass_utils import run_bass_kernel_spmd

    def arr(name):
        return np.asarray(inputs[name])

    def ones_row(w, bias):
        cols = w.shape[1]
        r = np.zeros((HC + 1, 2, cols), w.dtype)
        r[0:HC] = w.reshape(2, HC, cols).transpose(1, 0, 2)
        r[HC, 1] = bias
        return r.reshape(HC + 1, 2 * cols)

    x = arr("x").reshape(B, CIN, SIDE, PATCH, SIDE, PATCH).transpose(0, 2, 4, 3, 5, 1).reshape(B * T, DTOK)
    xp = np.zeros((NT * TT, DTOK), x.dtype)
    xp[0:B * T] = x
    w1 = arr("L0_ffn_w1")
    w1p = np.stack([ones_row(w1[e], arr("L0_ffn_b1")[e]) for e in range(E)], 1)
    w2 = arr("L0_ffn_w2")
    w2p = np.zeros((128, E, FC + 1, C), w2.dtype)
    w2p[:, :, 0:FC] = w2.reshape(E, FC, 128, C).transpose(2, 0, 1, 3)
    w2p[0, :, FC] = arr("L0_ffn_b2")
    key = np.arange(KEYS)
    ch = np.arange(C)
    tok = np.arange(TT)
    data = {
        "xt": xp.reshape(NT, TT, KT, 128).transpose(0, 3, 2, 1).reshape(NT, 128, KT * TT),
        "wtok": arr("L0_tok_W").reshape(KT, 128, C).transpose(1, 0, 2).reshape(128, KT * C),
        "wqkv": ones_row(arr("L0_attn_W_attn").T, arr("L0_attn_b_attn")),
        "wo": ones_row(arr("L0_attn_W_o").T, arr("L0_attn_b_o")),
        "wr": arr("L0_ffn_router_w").T.reshape(2, HC, E).transpose(1, 0, 2).reshape(HC, 2 * E),
        "w1": w1p.reshape(HC + 1, E * 2 * F),
        "w2": w2p.reshape(128, E * (FC + 1) * C),
        "idf": np.eye(128, dtype=np.float32),
        "idh": np.eye(128, dtype=np.float16),
        "selq": (np.arange(T)[:, None] == tok[None, :] % T).astype(ml_dtypes.bfloat16),
        "causal": np.where(np.arange(T)[:, None] >= np.arange(T)[None, :], 0.0, -1e30).astype(ml_dtypes.bfloat16),
        "selv": np.stack([tok[:, None] == b * T + key[None, :] % T for b in range(TI)], 1).reshape(TT, TI * KEYS).astype(np.float16),
        "hmask": np.repeat(np.arange(HC)[:, None] // HD == np.arange(HH)[None, :], TT, 1).astype(np.float16),
        "vmask": (key[:, None] // T == ch[None, :] // HD % GH).astype(np.float32),
        "vones": (key[:, None] // T == np.arange(GH)[None, :]).astype(np.float16),
        "before": (tok[:, None] < np.arange(128)[None, :]).astype(np.float16),
        "tileno": np.tile(np.arange(NS), (ST_, 1)).astype(np.float32),
        "tokens": (np.arange(NT)[None, :] * TT + tok[:, None]).astype(np.float32),
        "real": (tok[:, None] < LAST).astype(np.float32),
        "empty": np.concatenate([np.zeros((ST_, C)), B * T + np.arange(ST_)[:, None], -np.ones((ST_, 1)), np.zeros((ST_, 2))], 1).astype(np.float32),
        "eid": np.tile(np.arange(E), (TT, 1)).astype(np.float32),
    }
    nc = bacc.Bacc("TRN2", target_bir_lowering=False, num_devices=1)
    arrays, args = {}, []
    for name in ("eid", "before", "tileno", "tokens", "real", "empty"):
        data[name] = data.pop(name)
    for name, a in data.items():
        arrays[name] = np.ascontiguousarray(a)
        args.append(nc.dram_tensor(name, a.shape, mybir.dt.from_np(a.dtype), kind="ExternalInput").ap())
    args.append(nc.dram_tensor("slots", (NS * ST_, ROW), F32, kind="Internal").ap())
    args.append(nc.dram_tensor("out", (B * T + DUMP, C), F32, kind="ExternalOutput").ap())
    build(nc, *args)
    r = run_bass_kernel_spmd(nc, [arrays], core_ids=[0])
    return np.asarray(r.results[0]["out"])[0:B * T].reshape(B, T, C)
```
